# Optimizing a Trainium2 kernel written in Bass

```python
import numpy as np
import jax
import jax.numpy as jnp

def _softmax(x, axis=-1):
    return jax.nn.softmax(x, axis=axis)

def _gelu(x):
    return jax.nn.gelu(x, approximate=True)

def _silu(x):
    return jax.nn.silu(x)

def _sigmoid(x):
    return jax.nn.sigmoid(x)

def _layernorm(x, axis=-1, eps=1e-05):
    m = jnp.mean(x, axis=axis, keepdims=True)
    v = jnp.var(x, axis=axis, keepdims=True)
    return (x - m) / jnp.sqrt(v + eps)

def _scatter_add(tgt, idx, src, axis=0):
    return tgt.at[idx].add(src)

def _segment_sum(src, seg, n):
    return jax.ops.segment_sum(src, seg, n)
kernel_name = 'mk_seq_preln_d1_jaxref_r8_db8602'

def setup_inputs(seed: int=0):
    np.random.seed(seed)
    _w = jnp.asarray

    def _L0_attn_setup():
        import jax, jax.numpy as jnp
        import numpy as np
        key = jax.random.key(seed)
        ks = jax.random.split(key, 5)
        B, S, D = (1, 512, 256)
        H, Dh = (16, 128)
        scale = 1.0 / np.sqrt(D).astype(np.float32)
        return {'x': jax.random.normal(ks[0], (B, S, D), dtype=jnp.float32), 'W_K': jax.random.normal(ks[1], (H, Dh, D), dtype=jnp.float32) * scale, 'W_Q': jax.random.normal(ks[2], (H, Dh, D), dtype=jnp.float32) * scale, 'W_V': jax.random.normal(ks[3], (H, Dh, D), dtype=jnp.float32) * scale, 'W_O': jax.random.normal(ks[4], (D, H * Dh), dtype=jnp.float32) * scale}
    _L0_attn_in = _L0_attn_setup()

    def _L0_ffn_setup():
        import math
        import jax, jax.numpy as jnp
        import numpy as np
        DIM = 256
        RANK = 8
        B, T = (4, 512)

        def _orthogonal(key, n):
            a = jax.random.normal(key, (n, n), dtype=jnp.float32)
            q, r = jnp.linalg.qr(a)
            q = q * jnp.sign(jnp.diagonal(r))[None, :]
            return q
        key = jax.random.key(seed)
        kx, kf = jax.random.split(key)
        x = jax.random.normal(kx, (B, T, DIM), dtype=jnp.float32)
        fkeys = jax.random.split(kf, RANK)
        factors = jnp.stack([_orthogonal(fkeys[r], DIM) * (r + 1) ** (-0.5) for r in range(RANK)])
        bias = jnp.zeros((DIM,), dtype=jnp.float32)
        return {'x': x, 'factors': factors, 'bias': bias}
    _L0_ffn_in = _L0_ffn_setup()
    _d = {'L0_attn_x': _L0_attn_in['x'], 'L0_attn_W_K': _L0_attn_in['W_K'], 'L0_attn_W_Q': _L0_attn_in['W_Q'], 'L0_attn_W_V': _L0_attn_in['W_V'], 'L0_attn_W_O': _L0_attn_in['W_O'], 'L0_ffn_factors': _L0_ffn_in['factors'], 'L0_ffn_bias': _L0_ffn_in['bias']}
    _x0 = _d['L0_attn_x']
    _d['L0_attn_x'] = jax.random.normal(jax.random.fold_in(jax.random.key(seed), 1), (1, 2048, 256), dtype=_x0.dtype)
    del _x0
    return _d

def reference(L0_attn_x, L0_attn_W_K, L0_attn_W_Q, L0_attn_W_V, L0_attn_W_O, L0_ffn_factors, L0_ffn_bias):

    def _L0_attn_ref(x, W_K, W_Q, W_V, W_O):
        import jax, jax.numpy as jnp
        import numpy as np
        b, pos, d_model = x.shape
        d_head = W_K.shape[1]
        k = jnp.einsum('ihd,bpd->biph', W_K, x)
        q = jnp.einsum('ihd,bpd->biph', W_Q, x)
        v = jnp.einsum('ihd,bpd->biph', W_V, x)
        scores = jnp.einsum('biph,biqh->biqp', k, q)
        mask = jnp.tril(jnp.ones((pos, pos), dtype=x.dtype))
        masked = scores * mask - jnp.float32(10000000000.0) * (1.0 - mask)
        attn = jax.nn.softmax(masked / jnp.sqrt(jnp.float32(d_head)), axis=-1)
        z = jnp.einsum('biqp,biph->biqh', attn, v)
        z_flat = jnp.transpose(z, (0, 2, 1, 3)).reshape(b, pos, -1)
        out = jnp.einsum('df,bqf->bqd', W_O, z_flat)
        return out

    def _L0_ffn_ref(x, factors, bias):
        import math
        import jax, jax.numpy as jnp
        import numpy as np
        DIM = 256
        RANK = 8
        B, T = (4, 512)

        def _orthogonal(key, n):
            a = jax.random.normal(key, (n, n), dtype=jnp.float32)
            q, r = jnp.linalg.qr(a)
            q = q * jnp.sign(jnp.diagonal(r))[None, :]
            return q
        rank = factors.shape[0]
        mixed = jnp.einsum('btd,rde->bte', x, factors)
        mixed = mixed / math.sqrt(rank) + bias
        return mixed
    x = L0_attn_x
    x = x + _L0_attn_ref(_layernorm(x, axis=-1), L0_attn_W_K, L0_attn_W_Q, L0_attn_W_V, L0_attn_W_O)
    x = x + _L0_ffn_ref(_layernorm(x, axis=-1), L0_ffn_factors, L0_ffn_bias)
    return x

_drawn_inputs = setup_inputs


def setup_inputs(seed=0):
    import zlib

    import numpy as np

    out = dict(_drawn_inputs(seed))
    spreads = {'L0_ffn_bias': (0.0, 0.1)}
    factors = {}
    for name, (base, spread) in spreads.items():
        noise = np.random.default_rng([zlib.crc32(name.encode()), seed]).standard_normal(out[name].shape)
        drawn = base * np.exp(spread * noise) if base else spread * noise
        out[name] = jnp.asarray(drawn.astype(out[name].dtype))
    for name, factor in factors.items():
        out[name] = (out[name] * factor).astype(out[name].dtype)
    return out
```

```python
from contextlib import ExitStack

import numpy as np

import concourse.bass as bass
from concourse import mybir

ALU = mybir.AluOpType
ACT = mybir.ActivationFunctionType
AX = mybir.AxisListType
F32 = mybir.dt.float32
F16 = mybir.dt.float16
BF16 = mybir.dt.bfloat16
U32 = mybir.dt.uint32
RMAX = bass.bass_isa.ReduceOp.absmax

P = 128
BANK = 512
LN_EPS = 1e-5

X_SCALE = 2.0 ** 11
W_TOP = 2.0 ** 13
QKV_DOWN = 2.0 ** -18
P_SCALE = 2.0 ** 15
EXPONENT_BITS = 0x7F800000


def preln_attention_ffn(nc, x, w_k, w_q, w_v, w_o, factors, bias, out):
    S, D = x.shape[1], x.shape[2]
    H, Dh = w_k.shape[0], w_k.shape[1]
    R = factors.shape[0]
    QT = S // P
    KD = D // P
    NC = S // BANK
    TPC = BANK // P
    PAIRS = H // 2
    assert Dh == P and D == 2 * P and QT == 16 and H % 2 == 0

    LAG_T, LAG_PV, LAG_OUT = 1, 2, 3
    PRO = LAG_OUT
    SLOTS = 2 * QT
    LN_STEPS = 6
    ORDER = list(range(QT))

    PIECES = [("max", 0), ("spread", 0), ("wqk", 0), ("wvo", 0)]
    for c in range(NC):
        PIECES += [("k", c), ("q", c)]
    PIECES += [("v", c) for c in range(NC)]
    NP = len(PIECES)
    FIRST_PIECE = QT - NP
    KQ_PIECES = NP - NC

    def z_down(t):
        return 2.0 ** -(15 + int(np.ceil(np.log2((t + 1) * P))))

    def tile_of(k):
        return ORDER[k % QT]

    def par(k):
        return k % 2

    def hpar(k):
        return (k // QT) % 2

    def tiles(it, k):
        return it * SLOTS + (k + 1)

    NG = [-(-(t + 1) // 8) for t in range(QT)]
    NG_HEAD = sum(NG)

    def groups(it, k):
        return it * (2 * NG_HEAD) + ((k // QT) * NG_HEAD + sum(NG[ORDER[i]] for i in range(k % QT + 1)))

    def pieces(it, k, j):
        return it * (2 * NP) + (NP * (k // QT + 1) + j + 1)

    def pieces_before(it, k):
        if isinstance(it, int) and 2 * it + k // QT + 1 >= H:
            return NP * H
        return it * (2 * NP) + (NP * (k // QT + 1) + min(max(k % QT - FIRST_PIECE, 0), NP))

    def piece_of(it, k):
        if isinstance(it, int) and 2 * it + k // QT + 1 >= H:
            return None
        j = k % QT - FIRST_PIECE
        return j if 0 <= j < NP else None

    def exists(it, k):
        return not isinstance(it, int) or (k >= 0 and it * SLOTS + k < PAIRS * SLOTS)

    def next_head(it, k):
        return not (isinstance(it, int) and 2 * it + k // QT + 1 >= H)

    def run_slots(eng, slot):
        for k in range(PRO):
            slot(0, k)
        with eng.Fori(0, PAIRS - 1) as it:
            for k in range(PRO, PRO + SLOTS):
                slot(it, k)
        for k in range(PRO, SLOTS + LAG_OUT):
            slot(PAIRS - 1, k)

    S_BASE = []
    half = 0
    for t in ORDER:
        nb = -(-(t + 1) // TPC)
        if nb <= 2:
            S_BASE.append(2 * half)
            half ^= 1
        else:
            S_BASE.append(0)
            half = 0

    def s_banks(k):
        b = S_BASE[k % QT]
        return set(range(b, b + -(-(tile_of(k) + 1) // TPC)))

    def s_free_after(k):
        for d in range(1, QT):
            if s_banks(k - d + SLOTS) & s_banks(k):
                return k - d

    with ExitStack() as ctx:
        def sb(name, shape, dt):
            return ctx.enter_context(nc.sbuf_tensor(name, shape, dt))

        def ps(name, shape, dt):
            return ctx.enter_context(nc.psum_tensor(name, shape, dt))

        def sem(name):
            return ctx.enter_context(nc.semaphore(name))

        acc = sb("acc", [P, QT, D], F32)
        xt_hi = sb("xt_hi", [P, KD, S], F16)
        xt_lo = sb("xt_lo", [P, KD, S], F16)
        w_raw = sb("w_raw", [P, 4, D], F32)
        w_hi = sb("w_hi", [P, 3, KD, P], F16)
        w_lo = sb("w_lo", [P, 3, KD, P], F16)
        wo_hi = sb("wo_hi", [P, 2, D], F16)
        wo_lo = sb("wo_lo", [P, 2, D], F16)
        k_hi = sb("k_hi", [P, 2, S], F16)
        k_lo = sb("k_lo", [P, 2, S], F16)
        q_hi = sb("q_hi", [P, 2, S], F16)
        q_lo = sb("q_lo", [P, 2, S], F16)
        v_hi = sb("v_hi", [P, 2, QT, P], F16)
        v_lo = sb("v_lo", [P, 2, QT, P], F16)
        prob = sb("prob", [P, 2, S], F32)
        p_hi = sb("p_hi", [P, 2, S], F16)
        p_lo = sb("p_lo", [P, 2, S], F16)
        pt_hi = sb("pt_hi", [P, 2, QT, P], F16)
        pt_lo = sb("pt_lo", [P, 2, QT, P], F16)
        z_hi = sb("z_hi", [P, 2, P], F16)
        z_lo = sb("z_lo", [P, 2, P], F16)
        ident32 = sb("ident32", [P, P], F32)
        ident16 = sb("ident16", [P, P], F16)
        ident_b = sb("ident_b", [P, P], BF16)
        mask_b = sb("mask_b", [P, P], BF16)
        ones32 = sb("ones32", [P, P], F32)
        amax = sb("amax", [P, P], F32)
        amax_t = sb("amax_t", [P, P], F32)
        top = sb("top", [P, 1], F32)
        top_diag = sb("top_diag", [P, 4], F32)
        gmax = sb("gmax", [P, 4], F32)
        gclamp = sb("gclamp", [P, 4], F32)
        pow2 = sb("pow2", [P, 4], F32)
        w_inv = sb("w_inv", [P, 4], F32)
        w_scale = sb("w_scale", [P, 4], F32)
        c_score = sb("c_score", [P, 2], F32)
        c_out = sb("c_out", [P, 2], F32)
        neg_max = sb("neg_max", [P, 2], F32)
        exp_bias = sb("exp_bias", [P, 2], F32)
        row_sum = sb("row_sum", [P, 2], F32)
        row_rec = sb("row_rec", [P, 2], F32)
        out_scale = sb("out_scale", [P, 4], F32)
        stats = sb("stats", [P, QT, 6], F32)
        mean_var = sb("mean_var", [P, QT, 2], F32)
        var_eps = sb("var_eps", [P, QT], F32)
        std = sb("std", [P, QT], F32)
        rstd0 = sb("rstd0", [P, QT], F32)
        newton = sb("newton", [P, QT], F32)
        rstd = sb("rstd", [P, QT], F32)
        f_raw = sb("f_raw", [P, R, KD, D], F32)
        f_sum = sb("f_sum", [P, KD, D], F32)
        bias_row = sb("bias_row", [P, D], F32)
        x2t = sb("x2t", [P, 2, KD, P], F32)
        xn = prob[:, :, :].rearrange("p a (t d) -> p (a t) d", d=D)
        resid = sb("resid", [P, QT, D], F32)
        res = f_raw[:, :, :, :].rearrange("p r k e -> p (r k) e")

        s_ps = ps("s_ps", [P, 4, BANK], F32)
        t_hi = ps("t_hi", [P, 8, P], F16)
        t_lo = ps("t_lo", [P, 8, P], F16)
        z_ps = ps("z_ps", [P, BANK], F32)
        m_ps = ps("m_ps", [P, BANK], F32)

        x_loaded = [sem(f"x_loaded{c}") for c in range(NC)]
        w_loaded = sem("w_loaded")
        f_loaded = sem("f_loaded")
        consts_zero = sem("consts_zero")
        consts_ready = sem("consts_ready")
        stats_done = sem("stats_done")
        aggr_done = sem("aggr_done")
        ln_step = sem("ln_step")
        std_ready = sem("std_ready")
        xn_ready = sem("xn_ready")
        xt_full = sem("xt_full")
        xt_hi_done = sem("xt_hi_done")
        xt_lo_done = sem("xt_lo_done")
        amax_ready = sem("amax_ready")
        top_ready = sem("top_ready")
        scale_step = sem("scale_step")
        piece_full = sem("piece_full")
        piece_hi_done = sem("piece_hi_done")
        piece_lo_done = sem("piece_lo_done")
        scores_done = sem("scores_done")
        max_done = sem("max_done")
        bias_ready = sem("bias_ready")
        exp_done = sem("exp_done")
        rec_done = sem("rec_done")
        out_scale_ready = sem("out_scale_ready")
        p_hi_ready = sem("p_hi_ready")
        p_lo_ready = sem("p_lo_ready")
        t_hi_full = sem("t_hi_full")
        t_lo_full = sem("t_lo_full")
        pt_hi_ready = sem("pt_hi_ready")
        pt_lo_ready = sem("pt_lo_ready")
        pv_done = sem("pv_done")
        z_hi_ready = sem("z_hi_ready")
        z_lo_ready = sem("z_lo_ready")
        out_full = sem("out_full")
        acc_added = sem("acc_added")
        f_sum_step = sem("f_sum_step")
        resid_ready = sem("resid_ready")
        x2_full = sem("x2_full")
        x2t_ready = sem("x2t_ready")
        ffn_full = sem("ffn_full")
        res_ready = sem("res_ready")
        stored = sem("stored")

        x_dram = x.rearrange("b (t p) d -> p (b t) d", p=P)
        out_dram = out.rearrange("b (t p) d -> p (b t) d", p=P)
        wo_dram = w_o.rearrange("(k p) (i h) -> p k i h", p=P, h=Dh)
        f_dram = factors.rearrange("r (k p) e -> p r k e", p=P)

        block = ctx.enter_context(nc.Block())

        @block.sync
        def _(sp):
            def load_weights(head):
                for j, w in enumerate((w_q, w_k, w_v)):
                    sp.dma_start(w_raw[:, j, :], w[bass.ds(head, 1)].rearrange("i h d -> h (i d)")).then_inc(w_loaded, 16)
                sp.dma_start(w_raw[:, 3, :].rearrange("p (k h) -> p k h", k=KD),
                             wo_dram[:, :, bass.ds(head, 1), :].rearrange("p k i h -> p k (i h)")).then_inc(w_loaded, 16)

            for c in range(NC):
                sp.dma_start(acc[:, c * TPC:(c + 1) * TPC, :], x_dram[:, c * TPC:(c + 1) * TPC, :]).then_inc(x_loaded[c], 16)
            load_weights(0)
            sp.dma_start(f_raw[:, :, :, :].rearrange("p r k e -> p (r k) e"),
                         f_dram.rearrange("p r k e -> p (r k) e")).then_inc(f_loaded, 16)
            sp.dma_start(bias_row[:, :], bias.rearrange("(a d) -> a d", a=1).broadcast_to([P, D])).then_inc(f_loaded, 16)
            with sp.Fori(1, H) as head:
                sp.wait_ge(piece_full, head * NP + (4 - NP))
                load_weights(head)
            for c in range(NC):
                sp.wait_ge(res_ready, (c + 1) * TPC)
                sp.dma_start(out_dram[:, c * TPC:(c + 1) * TPC, :], res[:, c * TPC:(c + 1) * TPC, :]).then_inc(stored, 16)
            sp.wait_ge(stored, 16 * NC)

        @block.gpsimd
        def _(pool):
            for m in (ident32, ident16, ident_b, mask_b):
                nc.gpsimd.memset(m[:, :], 0.0).then_inc(consts_zero, 1)
            nc.gpsimd.memset(ones32[:, :], 1.0).then_inc(consts_ready, 1)
            nc.gpsimd.memset(amax[:, :], 0.0).then_inc(consts_ready, 1)
            pool.wait_ge(consts_zero, 4)
            for m in (ident32, ident16, ident_b):
                nc.gpsimd.affine_select(out=m[:, :], in_=m[:, :], compare_op=ALU.not_equal, fill=1.0, base=0,
                                        pattern=[[-1, P]], channel_multiplier=1).then_inc(consts_ready, 1)
            nc.gpsimd.affine_select(out=mask_b[:, :], in_=mask_b[:, :], compare_op=ALU.is_ge, fill=-3e38, base=0,
                                    pattern=[[-1, P]], channel_multiplier=1).then_inc(consts_ready, 1)

            pool.wait_ge(f_loaded, 32)
            for r in range(1, R):
                if r > 1:
                    pool.wait_ge(f_sum_step, r - 1)
                nc.gpsimd.tensor_tensor(out=f_sum[:, :, :], in0=f_raw[:, 0, :, :] if r == 1 else f_sum[:, :, :],
                                        in1=f_raw[:, r, :, :], op=ALU.add).then_inc(f_sum_step, 1)

            def slot(it, k):
                if exists(it, k):
                    w, pp = (tile_of(k) + 1) * P, par(k)
                    if exists(it, k - 2):
                        pool.wait_ge(t_lo_full, groups(it, k - 2))
                    pool.wait_ge(p_hi_ready, tiles(it, k))
                    nc.gpsimd.tensor_tensor(out=p_lo[:, pp, 0:w], in0=prob[:, pp, 0:w], in1=p_hi[:, pp, 0:w],
                                            op=ALU.subtract).then_inc(p_lo_ready, 1)

            run_slots(pool, slot)
            for t in range(QT):
                pool.wait_ge(acc_added, PAIRS * SLOTS)
                nc.gpsimd.tensor_tensor(out=resid[:, t, :], in0=acc[:, t, :], in1=bias_row[:, :],
                                        op=ALU.add).then_inc(resid_ready, 1)

        @block.tensor
        def _(pe):
            mm = nc.tensor.matmul

            pe.wait_ge(consts_ready, 6)
            n = 0
            for c in range(NC):
                pe.wait_ge(xn_ready, (c + 1) * TPC)
                for kd in range(KD):
                    if n >= 4:
                        pe.wait_ge(xt_hi_done, n - 3)
                        pe.wait_ge(xt_lo_done, n - 3)
                    for t in range(TPC):
                        last = nc.tensor.transpose(s_ps[:, n % 4, t * P:(t + 1) * P],
                                                   xn[:, c * TPC + t, kd * P:(kd + 1) * P], ident32[:, :])
                    last.then_inc(xt_full, 1)
                    n += 1

            def piece(j, hp):
                what, c = PIECES[j]
                if what == "max":
                    last = nc.tensor.transpose(m_ps[:, 0:P], amax[:, :], ident32[:, :])
                elif what == "spread":
                    last = mm(m_ps[:, 0:4], ones32[:, :], top_diag[:, :], start=True, stop=True)
                elif what in ("wqk", "wvo"):
                    for b in range(4):
                        last = nc.tensor.transpose(m_ps[:, b * P:(b + 1) * P],
                                                   w_raw[:, 2 * (what == "wvo") + b // 2, (b % 2) * P:(b % 2 + 1) * P],
                                                   ident32[:, :])
                elif what in "kq":
                    m = "qk".index(what)
                    n = 0
                    for wt, xt in ((w_hi, xt_hi), (w_hi, xt_lo), (w_lo, xt_hi)):
                        for kd in range(KD):
                            last = mm(m_ps[:, :], wt[:, m, kd, :], xt[:, kd, c * BANK:(c + 1) * BANK],
                                      start=(n == 0), stop=(n == 3 * KD - 1))
                            n += 1
                else:
                    for b in range(TPC):
                        t = c * TPC + b
                        n = 0
                        for xt, wt in ((xt_hi, w_hi), (xt_hi, w_lo), (xt_lo, w_hi)):
                            for kd in range(KD):
                                last = mm(m_ps[:, b * P:(b + 1) * P], xt[:, kd, t * P:(t + 1) * P], wt[:, 2, kd, :],
                                          start=(n == 0), stop=(n == 3 * KD - 1))
                                n += 1
                last.then_inc(piece_full, 1)
                return last

            pe.wait_ge(xt_hi_done, NC * KD)
            pe.wait_ge(xt_lo_done, NC * KD)
            for j in range(NP):
                if j > 0:
                    pe.wait_ge(piece_hi_done, j)
                    pe.wait_ge(piece_lo_done, j)
                if j == 0:
                    pe.wait_ge(amax_ready, 1)
                piece(j, 0)

            def slot(it, k):
                if exists(it, k):
                    t, hp = tile_of(k), hpar(k)
                    if k % QT == 0:
                        pe.wait_ge(piece_hi_done, pieces(it, k - QT, KQ_PIECES - 1))
                        pe.wait_ge(piece_lo_done, pieces(it, k - QT, KQ_PIECES - 1))
                    f = s_free_after(k)
                    if exists(it, f):
                        pe.wait_ge(exp_done, tiles(it, f))
                    nb = -(-(t + 1) // TPC)
                    b0 = S_BASE[k % QT]
                    cols = (t + 1) * P
                    tq = slice(t * P, (t + 1) * P)
                    for b in range(nb):
                        w = min(BANK, cols - b * BANK)
                        ks = slice(b * BANK, b * BANK + w)
                        mm(s_ps[:, b0 + b, 0:w], q_hi[:, hp, tq], k_hi[:, hp, ks], start=True, stop=False)
                        mm(s_ps[:, b0 + b, 0:w], q_hi[:, hp, tq], k_lo[:, hp, ks], start=False, stop=False)
                    for b in range(nb):
                        w = min(BANK, cols - b * BANK)
                        ks = slice(b * BANK, b * BANK + w)
                        mm(s_ps[:, b0 + b, 0:w], q_lo[:, hp, tq], k_hi[:, hp, ks], start=False, stop=(b < nb - 1))
                    w = cols - (nb - 1) * BANK
                    mm(s_ps[:, b0 + nb - 1, w - P:w], ident_b[:, :], mask_b[:, :],
                       start=False, stop=True).then_inc(scores_done, 1)
                ko = k - LAG_OUT
                if exists(it, ko):
                    pe.wait_ge(z_hi_ready, tiles(it, ko))
                    pe.wait_ge(z_lo_ready, tiles(it, ko))
                    pe.wait_ge(piece_hi_done, pieces_before(it, k))
                    pe.wait_ge(piece_lo_done, pieces_before(it, k))
                    zp, hp = par(ko), hpar(ko)
                    mm(m_ps[:, 0:D], z_hi[:, zp, :], wo_hi[:, hp, :], start=True, stop=False)
                    mm(m_ps[:, 0:D], z_hi[:, zp, :], wo_lo[:, hp, :], start=False, stop=False)
                    mm(m_ps[:, 0:D], z_lo[:, zp, :], wo_hi[:, hp, :], start=False, stop=True).then_inc(out_full, 1)
                kv = k - LAG_PV
                if exists(it, kv):
                    hp, pp = hpar(kv), par(kv)
                    pe.wait_ge(pt_hi_ready, groups(it, kv))
                    pe.wait_ge(pt_lo_ready, groups(it, kv))
                    if kv % QT == 0:
                        pe.wait_ge(piece_hi_done, pieces(it, kv - QT, NP - 1))
                        pe.wait_ge(piece_lo_done, pieces(it, kv - QT, NP - 1))
                    if exists(it, kv - 1):
                        pe.wait_ge(z_lo_ready, tiles(it, kv - 1))
                        pe.wait_ge(z_hi_ready, tiles(it, kv - 1))
                    n = tile_of(kv) + 1
                    for b in range(n):
                        mm(z_ps[:, 0:P], v_hi[:, hp, b, :], pt_hi[:, pp, b, :], start=(b == 0), stop=False)
                        mm(z_ps[:, 0:P], v_hi[:, hp, b, :], pt_lo[:, pp, b, :], start=False, stop=False)
                        last = mm(z_ps[:, 0:P], v_lo[:, hp, b, :], pt_hi[:, pp, b, :], start=False, stop=(b == n - 1))
                    last.then_inc(pv_done, 1)
                kt = k - LAG_T
                if exists(it, kt):
                    pp, t = par(kt), tile_of(kt)
                    for g in range(NG[t]):
                        for src, dst, ready, full, read in ((p_hi, t_hi, p_hi_ready, t_hi_full, pt_hi_ready),
                                                            (p_lo, t_lo, p_lo_ready, t_lo_full, pt_lo_ready)):
                            if g == 0:
                                pe.wait_ge(ready, tiles(it, kt))
                            before = groups(it, kt) + (g - NG[t])
                            if not (isinstance(before, int) and before <= 0):
                                pe.wait_ge(read, before)
                            for b in range(8 * g, min(8 * g + 8, t + 1)):
                                last = nc.tensor.transpose(dst[:, b % 8, :], src[:, pp, b * P:(b + 1) * P], ident16[:, :])
                            last.then_inc(full, 1)
                j = piece_of(it, k)
                if j is not None:
                    if exists(it, ko):
                        pe.wait_ge(acc_added, tiles(it, ko))
                    pe.wait_ge(piece_hi_done, pieces_before(it, k))
                    pe.wait_ge(piece_lo_done, pieces_before(it, k))
                    if j == 0:
                        pe.wait_ge(amax_ready, it * 2 + (k // QT + 2))
                    piece(j, 1 - hpar(k))

            run_slots(pe, slot)

            def ffn(t):
                pe.wait_ge(x2t_ready, t + 1)
                if t >= 2:
                    pe.wait_ge(res_ready, t - 1)
                for kd in range(KD):
                    last = mm(s_ps[:, 2 + t % 2, 0:D], x2t[:, t % 2, kd, :], f_sum[:, kd, :],
                              start=(kd == 0), stop=(kd == KD - 1))
                last.then_inc(ffn_full, 1)

            pe.wait_ge(f_sum_step, R - 1)
            for t in range(QT):
                pe.wait_ge(xn_ready, QT + t + 1)
                if t >= 2:
                    pe.wait_ge(x2t_ready, t - 1)
                for kd in range(KD):
                    last = nc.tensor.transpose(s_ps[:, t % 2, kd * P:(kd + 1) * P], xn[:, t, kd * P:(kd + 1) * P],
                                               ident32[:, :])
                last.then_inc(x2_full, 1)
                if t >= 1:
                    ffn(t - 1)
            ffn(QT - 1)

        @block.scalar
        def _(act):
            act.wait_ge(ln_step, 1)
            nc.scalar.activation(std[:, :], var_eps[:, :], ACT.Sqrt).then_inc(std_ready, 1)
            for n in range(NC * KD):
                c, kd = n // KD, n % KD
                act.wait_ge(xt_full, n + 1)
                nc.scalar.copy(xt_hi[:, kd, c * BANK:(c + 1) * BANK], s_ps[:, n % 4, :]).then_inc(xt_hi_done, 1)

            def piece_hi(j, hp, full):
                act.wait_ge(piece_full, full)
                what, c = PIECES[j]
                if what == "max":
                    nc.scalar.copy(amax_t[:, :], m_ps[:, 0:P]).then_inc(piece_hi_done, 1)
                elif what == "spread":
                    nc.scalar.copy(gmax[:, :], m_ps[:, 0:4]).then_inc(piece_hi_done, 1)
                elif what == "wqk":
                    nc.scalar.mul(w_hi[:, 0, :, :], m_ps[:, 0:D], w_scale[:, 0:1])
                    nc.scalar.mul(w_hi[:, 1, :, :], m_ps[:, D:2 * D], w_scale[:, 1:2]).then_inc(piece_hi_done, 1)
                elif what == "wvo":
                    nc.scalar.mul(w_hi[:, 2, :, :], m_ps[:, 0:D], w_scale[:, 2:3])
                    nc.scalar.mul(wo_hi[:, hp, :], m_ps[:, D:2 * D], w_scale[:, 3:4]).then_inc(piece_hi_done, 1)
                else:
                    if what == "v":
                        dst = v_hi[:, hp, c * TPC:(c + 1) * TPC, :]
                    else:
                        dst = (k_hi if what == "k" else q_hi)[:, hp, c * BANK:(c + 1) * BANK]
                    nc.scalar.mul(dst, m_ps[:, :], QKV_DOWN).then_inc(piece_hi_done, 1)

            for j in range(NP):
                piece_hi(j, 0, j + 1)

            def slot(it, k):
                if exists(it, k):
                    w = (tile_of(k) + 1) * P
                    b0, pp = S_BASE[k % QT], par(k)
                    act.wait_ge(bias_ready, tiles(it, k))
                    nc.scalar.activation(prob[:, pp, 0:w], s_ps[:, :, :].rearrange("p b n -> p (b n)")[:, b0 * BANK:b0 * BANK + w],
                                         ACT.Exp, bias=exp_bias[:, pp:pp + 1], scale=c_score[:, hpar(k):hpar(k) + 1],
                                         accum_out=row_sum[:, pp:pp + 1]).then_inc(exp_done, 1)
                kt = k - LAG_T
                if exists(it, kt):
                    pp, t = par(kt), tile_of(kt)
                    for g in range(NG[t]):
                        act.wait_ge(t_lo_full, groups(it, kt) + (g + 1 - NG[t]))
                        n = min(8, t + 1 - 8 * g)
                        nc.scalar.copy(pt_lo[:, pp, 8 * g:8 * g + n, :], t_lo[:, 0:n, :]).then_inc(pt_lo_ready, 1)
                j = piece_of(it, k)
                if j is not None:
                    piece_hi(j, 1 - hpar(k), pieces(it, k, j))

            run_slots(act, slot)

            act.wait_ge(ln_step, LN_STEPS + 1)
            nc.scalar.activation(std[:, :], var_eps[:, :], ACT.Sqrt).then_inc(std_ready, 1)
            for t in range(QT):
                act.wait_ge(x2_full, t + 1)
                if t >= 2:
                    act.wait_ge(ffn_full, t - 1)
                nc.scalar.copy(x2t[:, t % 2, :, :], s_ps[:, t % 2, 0:D]).then_inc(x2t_ready, 1)

        @block.vector
        def _(dve):
            v = nc.vector

            def layernorm_rows(call, scale):
                for t in range(QT):
                    if call == 0 and t % TPC == 0:
                        dve.wait_ge(x_loaded[t // TPC], 16)
                    if call == 1:
                        dve.wait_ge(acc_added, PAIRS * SLOTS - QT + ORDER.index(t) + 1)
                    v.bn_stats(stats[:, t, :], acc[:, t, :]).then_inc(stats_done, 1)
                for t in range(QT):
                    dve.wait_ge(stats_done, call * QT + t + 1)
                    v.bn_aggr(mean_var[:, t, :], stats[:, t, :]).then_inc(aggr_done, 1)
                dve.wait_ge(aggr_done, (call + 1) * QT)
                n = call * LN_STEPS
                v.tensor_scalar(var_eps[:, :], mean_var[:, :, 1], LN_EPS, None, ALU.add).then_inc(ln_step, 1)
                dve.wait_ge(std_ready, call + 1)
                v.reciprocal(rstd0[:, :], std[:, :]).then_inc(ln_step, 1)
                dve.wait_ge(ln_step, n + 2)
                v.tensor_tensor(newton[:, :], rstd0[:, :], rstd0[:, :], ALU.mult).then_inc(ln_step, 1)
                dve.wait_ge(ln_step, n + 3)
                v.tensor_tensor(std[:, :], newton[:, :], var_eps[:, :], ALU.mult).then_inc(ln_step, 1)
                dve.wait_ge(ln_step, n + 4)
                v.tensor_scalar(newton[:, :], std[:, :], -0.5 * scale, 1.5 * scale, ALU.mult, ALU.add).then_inc(ln_step, 1)
                dve.wait_ge(ln_step, n + 5)
                v.tensor_tensor(rstd[:, :], newton[:, :], rstd0[:, :], ALU.mult).then_inc(ln_step, 1)
                dve.wait_ge(ln_step, n + 6)
                for t in range(QT):
                    v.tensor_scalar(xn[:, t, :], acc[:, t, :], mean_var[:, t, 0:1], rstd[:, t:t + 1],
                                    ALU.subtract, ALU.mult).then_inc(xn_ready, 1)

            def head_amax(count):
                dve.wait_ge(w_loaded, count * 64)
                v.tensor_reduce(amax[:, 0:4], w_raw[:, :, :], AX.X, ALU.max,
                                apply_absolute_value=True).then_inc(amax_ready, 1)

            def head_scales(count, hp):
                n = count * 3 - 3
                v.tensor_scalar(gclamp[:, :], gmax[:, :], 1e-30, None, ALU.max).then_inc(scale_step, 1)
                dve.wait_ge(scale_step, n + 1)
                v.tensor_scalar(pow2[:, :].bitcast(U32), gclamp[:, :].bitcast(U32), EXPONENT_BITS, None,
                                ALU.bitwise_and).then_inc(scale_step, 1)
                dve.wait_ge(scale_step, n + 2)
                v.tensor_scalar(w_inv[:, :], pow2[:, :], 1.0 / W_TOP, None, ALU.mult).then_inc(scale_step, 1)
                dve.wait_ge(scale_step, n + 3)
                v.scalar_tensor_tensor(c_score[:, hp:hp + 1], w_inv[:, 0:1],
                                       float(Dh) ** -0.5 / (X_SCALE * QKV_DOWN) ** 2, w_inv[:, 1:2],
                                       ALU.mult, ALU.mult)
                v.scalar_tensor_tensor(c_out[:, hp:hp + 1], w_inv[:, 2:3], 1.0 / (X_SCALE * QKV_DOWN), w_inv[:, 3:4],
                                       ALU.mult, ALU.mult)
                v.reciprocal(w_scale[:, :], w_inv[:, :]).then_inc(piece_lo_done, 1)

            def piece_lo(j, hp, done, count):
                dve.wait_ge(piece_hi_done, done)
                what, c = PIECES[j]
                if what == "max":
                    v.tensor_reduce(top[:, :], amax_t[:, :], AX.X, ALU.max).then_inc(top_ready, 1)
                    dve.wait_ge(top_ready, count)
                    v.tensor_scalar(top_diag[:, :], ident32[:, 0:4], top[:, 0:1], None, ALU.mult).then_inc(piece_lo_done, 1)
                    return
                if what == "spread":
                    head_scales(count, hp)
                    return
                if what in ("wqk", "wvo"):
                    for m in range(2):
                        i = 2 * (what == "wvo") + m
                        hi, lo = (wo_hi[:, hp, :], wo_lo[:, hp, :]) if i == 3 else (
                            w_hi[:, i, :, :].rearrange("p k h -> p (k h)"), w_lo[:, i, :, :].rearrange("p k h -> p (k h)"))
                        last = v.scalar_tensor_tensor(lo, m_ps[:, m * D:(m + 1) * D], w_scale[:, i:i + 1], hi,
                                                      ALU.mult, ALU.subtract)
                else:
                    if what == "v":
                        hi, lo = (a[:, hp, c * TPC:(c + 1) * TPC, :].rearrange("p t h -> p (t h)") for a in (v_hi, v_lo))
                    else:
                        hi, lo = (a[:, hp, c * BANK:(c + 1) * BANK] for a in ((k_hi, k_lo) if what == "k" else (q_hi, q_lo)))
                    last = v.scalar_tensor_tensor(lo, m_ps[:, :], QKV_DOWN, hi, ALU.mult, ALU.subtract)
                last.then_inc(piece_lo_done, 1)

            layernorm_rows(0, X_SCALE)
            dve.wait_ge(consts_ready, 6)
            head_amax(1)
            for n in range(NC * KD):
                c, kd = n // KD, n % KD
                dve.wait_ge(xt_hi_done, n + 1)
                v.tensor_tensor(xt_lo[:, kd, c * BANK:(c + 1) * BANK], s_ps[:, n % 4, :],
                                xt_hi[:, kd, c * BANK:(c + 1) * BANK], ALU.subtract).then_inc(xt_lo_done, 1)
            for j in range(NP):
                piece_lo(j, 0, j + 1, 1)

            def slot(it, k):
                if k % QT == 0 and exists(it, k) and next_head(it, k):
                    head_amax(it * 2 + (k // QT + 2))
                if exists(it, k):
                    w, pp, b0 = (tile_of(k) + 1) * P, par(k), S_BASE[k % QT]
                    dve.wait_ge(scores_done, tiles(it, k))
                    v.tensor_reduce(neg_max[:, pp:pp + 1], s_ps[:, :, :].rearrange("p b n -> p (b n)")[:, b0 * BANK:b0 * BANK + w],
                                    AX.X, ALU.max, negate=True).then_inc(max_done, 1)
                    dve.wait_ge(max_done, tiles(it, k))
                    v.tensor_scalar(exp_bias[:, pp:pp + 1], neg_max[:, pp:pp + 1], c_score[:, hpar(k):hpar(k) + 1],
                                    float(np.log(P_SCALE)), ALU.mult, ALU.add).then_inc(bias_ready, 1)
                ko = k - LAG_OUT
                if exists(it, ko):
                    dve.wait_ge(out_full, tiles(it, ko))
                    dve.wait_ge(out_scale_ready, tiles(it, ko))
                    t = tile_of(ko)
                    v.scalar_tensor_tensor(acc[:, t, :], m_ps[:, 0:D], out_scale[:, ko % 4:ko % 4 + 1], acc[:, t, :],
                                           ALU.mult, ALU.add).then_inc(acc_added, 1)
                kv = k - LAG_PV
                if exists(it, kv):
                    zp, down = par(kv), z_down(tile_of(kv))
                    dve.wait_ge(pv_done, tiles(it, kv))
                    v.tensor_scalar(z_hi[:, zp, :], z_ps[:, 0:P], down, None, ALU.mult).then_inc(z_hi_ready, 1)
                    dve.wait_ge(z_hi_ready, tiles(it, kv))
                    v.scalar_tensor_tensor(z_lo[:, zp, :], z_ps[:, 0:P], down, z_hi[:, zp, :],
                                           ALU.mult, ALU.subtract).then_inc(z_lo_ready, 1)
                kt = k - LAG_T
                if exists(it, kt):
                    pp, t = par(kt), tile_of(kt)
                    for g in range(NG[t]):
                        dve.wait_ge(t_hi_full, groups(it, kt) + (g + 1 - NG[t]))
                        n = min(8, t + 1 - 8 * g)
                        v.tensor_copy(pt_hi[:, pp, 8 * g:8 * g + n, :], t_hi[:, 0:n, :]).then_inc(pt_hi_ready, 1)
                j = piece_of(it, k)
                if j is not None:
                    piece_lo(j, 1 - hpar(k), pieces(it, k, j), it * 2 + (k // QT + 2))
                if exists(it, k):
                    w, pp, hp = (tile_of(k) + 1) * P, par(k), hpar(k)
                    dve.wait_ge(exp_done, tiles(it, k))
                    v.tensor_copy(p_hi[:, pp, 0:w], prob[:, pp, 0:w]).then_inc(p_hi_ready, 1)
                    v.reciprocal(row_rec[:, pp:pp + 1], row_sum[:, pp:pp + 1]).then_inc(rec_done, 1)
                    dve.wait_ge(rec_done, tiles(it, k))
                    v.scalar_tensor_tensor(out_scale[:, k % 4:k % 4 + 1], row_rec[:, pp:pp + 1], 1.0 / z_down(tile_of(k)),
                                           c_out[:, hp:hp + 1], ALU.mult, ALU.mult).then_inc(out_scale_ready, 1)

            run_slots(dve, slot)

            layernorm_rows(1, 1.0)
            for t in range(QT):
                dve.wait_ge(ffn_full, t + 1)
                if t == 0:
                    dve.wait_ge(resid_ready, QT)
                v.scalar_tensor_tensor(res[:, t, :], s_ps[:, 2 + t % 2, 0:D], float(R) ** -0.5, resid[:, t, :],
                                       ALU.mult, ALU.add).then_inc(res_ready, 1)


_INS = ["L0_attn_x", "L0_attn_W_K", "L0_attn_W_Q", "L0_attn_W_V", "L0_attn_W_O", "L0_ffn_factors", "L0_ffn_bias"]


def kernel(**inputs):
    from concourse.bacc import Bacc
    from concourse.bass_utils import run_bass_kernel_spmd

    nc = Bacc("TRN2", target_bir_lowering=False, num_devices=1)
    arrays, args = {}, []
    for name in _INS:
        a = np.ascontiguousarray(inputs[name])
        arrays[f"in_{name}"] = a
        args.append(nc.dram_tensor(f"in_{name}", a.shape, mybir.dt.from_np(a.dtype), kind="ExternalInput").ap())
    out = nc.dram_tensor("out_x", inputs["L0_attn_x"].shape, F32, kind="ExternalOutput").ap()
    preln_attention_ffn(nc, *args, out)
    r = run_bass_kernel_spmd(nc, [arrays], core_ids=[0])
    return r.results[0]["out_x"]
```

```python
from contextlib import ExitStack

import numpy as np

import concourse.bass as bass
from concourse import mybir

ALU = mybir.AluOpType
ACT = mybir.ActivationFunctionType
AX = mybir.AxisListType
F32 = mybir.dt.float32
F16 = mybir.dt.float16
BF16 = mybir.dt.bfloat16
U32 = mybir.dt.uint32
RMAX = bass.bass_isa.ReduceOp.absmax

P = 128
BANK = 512
LN_EPS = 1e-5

X_SCALE = 2.0 ** 11
W_TOP = 2.0 ** 13
QKV_DOWN = 2.0 ** -18
P_SCALE = 2.0 ** 15
EXPONENT_BITS = 0x7F800000


def preln_attention_ffn(nc, x, w_k, w_q, w_v, w_o, factors, bias, out):
    S, D = x.shape[1], x.shape[2]
    H, Dh = w_k.shape[0], w_k.shape[1]
    R = factors.shape[0]
    QT = S // P
    KD = D // P
    NC = S // BANK
    TPC = BANK // P
    PAIRS = H // 2
    assert Dh == P and D == 2 * P and QT == 16 and H % 2 == 0

    LAG_HI, LAG_T, LAG_PV, LAG_OUT = 1, 2, 3, 4
    PRO = LAG_OUT
    SLOTS = 2 * QT
    LN2_PARTS = [(0, QT - LAG_OUT), (QT - LAG_OUT, QT)]
    LN_STEPS = 6
    ORDER = [t for i in range(QT // 2) for t in (QT - 1 - i, i)]

    PIECES = [("max", 0), ("spread", 0), ("wqk", 0), ("wvo", 0)]
    for c in range(NC):
        PIECES += [("k", c), ("q", c)]
    PIECES += [("v", c) for c in range(NC)]
    NP = len(PIECES)
    FIRST_PIECE = QT - NP
    KQ_PIECES = NP - NC
    W_PIECES = 4

    def z_down(t):
        return 2.0 ** -(15 + int(np.ceil(np.log2((t + 1) * P))))

    def tile_of(k):
        return ORDER[k % QT]

    def par(k):
        return k % 2

    def hpar(k):
        return (k // QT) % 2

    def tiles(it, k):
        return it * SLOTS + (k + 1)

    SPLIT_HEAD = sum(t >= 2 * TPC for t in ORDER)

    def halves(it, k):
        return it * (2 * SPLIT_HEAD) + ((k // QT) * SPLIT_HEAD + sum(ORDER[i] >= 2 * TPC for i in range(k % QT + 1)))

    GROUPS = [[range(t + 1)] if t < 8 else [range(G0), range(G0, t + 1)] for t in range(QT) for G0 in [(t + 1) // 2]]
    NG = [len(g) for g in GROUPS]
    NG_HEAD = sum(NG)

    def groups(it, k):
        return it * (2 * NG_HEAD) + ((k // QT) * NG_HEAD + sum(NG[ORDER[i]] for i in range(k % QT + 1)))

    def pieces(it, k, j):
        return it * (2 * NP) + (NP * (k // QT + 1) + j + 1)

    def pieces_before(it, k):
        if isinstance(it, int) and 2 * it + k // QT + 1 >= H:
            return NP * H
        return it * (2 * NP) + (NP * (k // QT + 1) + min(max(k % QT - FIRST_PIECE, 0), NP))

    def piece_of(it, k):
        if isinstance(it, int) and 2 * it + k // QT + 1 >= H:
            return None
        j = k % QT - FIRST_PIECE
        return j if 0 <= j < NP else None

    def exists(it, k):
        return not isinstance(it, int) or (k >= 0 and it * SLOTS + k < PAIRS * SLOTS)

    def next_head(it, k):
        return not (isinstance(it, int) and 2 * it + k // QT + 1 >= H)

    def ffn_steps(it, k):
        if isinstance(it, int) and it == PAIRS - 1 and k > SLOTS:
            a = 4 * (k - SLOTS - 1)
            return range(a, a + 4)
        return range(0)

    def run_slots(eng, slot):
        for k in range(PRO):
            slot(0, k)
        with eng.Fori(0, PAIRS - 1) as it:
            for k in range(PRO, PRO + SLOTS):
                slot(it, k)
        for k in range(PRO, SLOTS + LAG_OUT):
            slot(PAIRS - 1, k)

    S_BASE = [{1: 3, 2: 2, 3: 0, 4: 0}[-(-(t + 1) // TPC)] for t in ORDER]

    def s_banks(k):
        b = S_BASE[k % QT]
        return set(range(b, b + -(-(tile_of(k) + 1) // TPC)))

    def s_free_after(k):
        for d in range(1, QT):
            if s_banks(k - d + SLOTS) & s_banks(k):
                return k - d

    with ExitStack() as ctx:
        def sb(name, shape, dt):
            return ctx.enter_context(nc.sbuf_tensor(name, shape, dt))

        def ps(name, shape, dt):
            return ctx.enter_context(nc.psum_tensor(name, shape, dt))

        def sem(name):
            return ctx.enter_context(nc.semaphore(name))

        acc = sb("acc", [P, QT, D], F32)
        xt_hi = sb("xt_hi", [P, KD, S], F16)
        xt_lo = sb("xt_lo", [P, KD, S], F16)
        w_raw = sb("w_raw", [P, 4, D], F32)
        w_hi = sb("w_hi", [P, 3, KD, P], F16)
        w_lo = sb("w_lo", [P, 3, KD, P], F16)
        wo_hi = sb("wo_hi", [P, 2, D], F16)
        wo_lo = sb("wo_lo", [P, 2, D], F16)
        k_hi = sb("k_hi", [P, 2, S], F16)
        k_lo = sb("k_lo", [P, 2, S], F16)
        q_hi = sb("q_hi", [P, 2, S], F16)
        q_lo = sb("q_lo", [P, 2, S], F16)
        v_hi = sb("v_hi", [P, 2, QT, P], F16)
        v_lo = sb("v_lo", [P, 2, QT, P], F16)
        prob = sb("prob", [P, 2, S], F32)
        p_hi = sb("p_hi", [P, 2, S], F16)
        p_lo = sb("p_lo", [P, 2, S], F16)
        pt_hi = sb("pt_hi", [P, 2, QT, P], F16)
        pt_lo = sb("pt_lo", [P, 2, QT, P], F16)
        z_hi = sb("z_hi", [P, 2, P], F16)
        z_lo = sb("z_lo", [P, 2, P], F16)
        ident32 = sb("ident32", [P, P], F32)
        ident16 = sb("ident16", [P, P], F16)
        ident_b = sb("ident_b", [P, P], BF16)
        mask_b = sb("mask_b", [P, P], BF16)
        ones32 = sb("ones32", [P, P], F32)
        amax = sb("amax", [P, P], F32)
        amax_t = sb("amax_t", [P, P], F32)
        top = sb("top", [P, 1], F32)
        top_diag = sb("top_diag", [P, 4], F32)
        gmax = sb("gmax", [P, 4], F32)
        gclamp = sb("gclamp", [P, 4], F32)
        pow2 = sb("pow2", [P, 4], F32)
        w_inv = sb("w_inv", [P, 4], F32)
        w_scale = sb("w_scale", [P, 4], F32)
        c_score = sb("c_score", [P, 2], F32)
        c_out = sb("c_out", [P, 2], F32)
        neg_max = sb("neg_max", [P, 2], F32)
        neg_max_half = sb("neg_max_half", [P, 2], F32)
        exp_bias = sb("exp_bias", [P, 2], F32)
        row_sum = sb("row_sum", [P, 2], F32)
        row_rec = sb("row_rec", [P, 2], F32)
        out_scale = sb("out_scale", [P, 4], F32)
        stats = sb("stats", [P, QT, 6], F32)
        mean_var = sb("mean_var", [P, QT, 2], F32)
        var_eps = sb("var_eps", [P, QT], F32)
        std = sb("std", [P, QT], F32)
        rstd0 = sb("rstd0", [P, QT], F32)
        newton = sb("newton", [P, QT], F32)
        rstd = sb("rstd", [P, QT], F32)
        f_raw = sb("f_raw", [P, R, KD, D], F32)
        f_sum = sb("f_sum", [P, KD, D], F32)
        bias_row = sb("bias_row", [P, D], F32)
        x2t = sb("x2t", [P, 2, KD, P], F32)
        xn = prob[:, :, :].rearrange("p a (t d) -> p (a t) d", d=D)
        resid = sb("resid", [P, QT, D], F32)
        f_rows = f_raw[:, :, :, :].rearrange("p r k e -> p (r k) e")
        xn2 = f_rows
        res = f_rows

        s_ps = ps("s_ps", [P, 4, BANK], F32)
        t_hi = ps("t_hi", [P, 8, P], F16)
        t_lo = ps("t_lo", [P, 8, P], F16)
        z_ps = ps("z_ps", [P, BANK], F32)
        m_ps = ps("m_ps", [P, BANK], F32)
        t_f32 = [t[:, :, :].rearrange("p b q -> p (b q)").bitcast(F32) for t in (t_hi, t_lo)]

        def head0_bank(j):
            if j < W_PIECES:
                return m_ps[:, :]
            if j < KQ_PIECES:
                return s_ps[:, j % 4, :]
            return [m_ps[:, :], z_ps[:, :], t_f32[0], t_f32[1]][j - KQ_PIECES]

        x_loaded = [sem(f"x_loaded{c}") for c in range(NC)]
        w_loaded = sem("w_loaded")
        f_loaded = sem("f_loaded")
        consts_zero = sem("consts_zero")
        consts_ready = sem("consts_ready")
        stats_done = sem("stats_done")
        aggr_done = sem("aggr_done")
        ln_step = sem("ln_step")
        std_ready = sem("std_ready")
        xn_ready = sem("xn_ready")
        xt_full = sem("xt_full")
        xt_hi_done = sem("xt_hi_done")
        xt_lo_done = sem("xt_lo_done")
        amax_ready = sem("amax_ready")
        top_ready = sem("top_ready")
        scale_step = sem("scale_step")
        piece_full = sem("piece_full")
        piece_hi_done = sem("piece_hi_done")
        piece_lo_done = sem("piece_lo_done")
        scores_done = sem("scores_done")
        scores_half = sem("scores_half")
        max_done = sem("max_done")
        bias_ready = sem("bias_ready")
        exp_done = sem("exp_done")
        rec_done = sem("rec_done")
        out_scale_ready = sem("out_scale_ready")
        p_hi_ready = sem("p_hi_ready")
        p_lo_ready = sem("p_lo_ready")
        t_hi_full = sem("t_hi_full")
        t_lo_full = sem("t_lo_full")
        pt_hi_ready = sem("pt_hi_ready")
        pt_lo_ready = sem("pt_lo_ready")
        pv_done = sem("pv_done")
        z_hi_ready = sem("z_hi_ready")
        z_lo_ready = sem("z_lo_ready")
        out_full = sem("out_full")
        acc_added = sem("acc_added")
        f_sum_step = sem("f_sum_step")
        resid_ready = sem("resid_ready")
        x2_full = sem("x2_full")
        x2t_ready = sem("x2t_ready")
        ffn_full = sem("ffn_full")
        res_ready = sem("res_ready")
        stored = sem("stored")

        x_dram = x.rearrange("b (t p) d -> p (b t) d", p=P)
        out_dram = out.rearrange("b (t p) d -> p (b t) d", p=P)
        wo_dram = w_o.rearrange("(k p) (i h) -> p k i h", p=P, h=Dh)
        f_dram = factors.rearrange("r (k p) e -> p r k e", p=P)

        block = ctx.enter_context(nc.Block())

        @block.sync
        def _(sp):
            def load_weights(head):
                for j, w in enumerate((w_q, w_k, w_v)):
                    sp.dma_start(w_raw[:, j, :], w[bass.ds(head, 1)].rearrange("i h d -> h (i d)")).then_inc(w_loaded, 16)
                sp.dma_start(w_raw[:, 3, :].rearrange("p (k h) -> p k h", k=KD),
                             wo_dram[:, :, bass.ds(head, 1), :].rearrange("p k i h -> p k (i h)")).then_inc(w_loaded, 16)

            load_weights(0)
            for c in range(NC):
                sp.dma_start(acc[:, c * TPC:(c + 1) * TPC, :], x_dram[:, c * TPC:(c + 1) * TPC, :]).then_inc(x_loaded[c], 16)
            sp.dma_start(f_raw[:, :, :, :].rearrange("p r k e -> p (r k) e"),
                         f_dram.rearrange("p r k e -> p (r k) e")).then_inc(f_loaded, 16)
            sp.dma_start(bias_row[:, :], bias.rearrange("(a d) -> a d", a=1).broadcast_to([P, D])).then_inc(f_loaded, 16)
            with sp.Fori(1, H) as head:
                sp.wait_ge(piece_full, head * NP + (4 - NP))
                load_weights(head)
            for i, t in enumerate(ORDER):
                sp.wait_ge(res_ready, i + 1)
                sp.dma_start(out_dram[:, t, :], res[:, t, :]).then_inc(stored, 16)
            sp.wait_ge(stored, 16 * QT)

        @block.gpsimd
        def _(pool):
            for m in (ident32, ident16, ident_b, mask_b):
                nc.gpsimd.memset(m[:, :], 0.0).then_inc(consts_zero, 1)
            nc.gpsimd.memset(ones32[:, :], 1.0).then_inc(consts_ready, 1)
            nc.gpsimd.memset(amax[:, :], 0.0).then_inc(consts_ready, 1)
            pool.wait_ge(consts_zero, 4)
            for m in (ident32, ident16, ident_b):
                nc.gpsimd.affine_select(out=m[:, :], in_=m[:, :], compare_op=ALU.not_equal, fill=1.0, base=0,
                                        pattern=[[-1, P]], channel_multiplier=1).then_inc(consts_ready, 1)
            nc.gpsimd.affine_select(out=mask_b[:, :], in_=mask_b[:, :], compare_op=ALU.is_ge, fill=-3e38, base=0,
                                    pattern=[[-1, P]], channel_multiplier=1).then_inc(consts_ready, 1)

            pool.wait_ge(f_loaded, 32)
            for r in range(1, R):
                if r > 1:
                    pool.wait_ge(f_sum_step, r - 1)
                nc.gpsimd.tensor_tensor(out=f_sum[:, :, :], in0=f_raw[:, 0, :, :] if r == 1 else f_sum[:, :, :],
                                        in1=f_raw[:, r, :, :], op=ALU.add).then_inc(f_sum_step, 1)

            def slot(it, k):
                if exists(it, k):
                    w, pp = (tile_of(k) + 1) * P, par(k)
                    if exists(it, k - 2):
                        pool.wait_ge(t_lo_full, groups(it, k - 2))
                    pool.wait_ge(p_hi_ready, tiles(it, k))
                    nc.gpsimd.tensor_tensor(out=p_lo[:, pp, 0:w], in0=prob[:, pp, 0:w], in1=p_hi[:, pp, 0:w],
                                            op=ALU.subtract).then_inc(p_lo_ready, 1)

            run_slots(pool, slot)
            for i, t in enumerate(ORDER):
                pool.wait_ge(acc_added, PAIRS * SLOTS - QT + i + 1)
                nc.gpsimd.tensor_tensor(out=resid[:, t, :], in0=acc[:, t, :], in1=bias_row[:, :],
                                        op=ALU.add).then_inc(resid_ready, 1)

        @block.tensor
        def _(pe):
            mm = nc.tensor.matmul

            def piece(j, m_ps=m_ps[:, :]):
                what, c = PIECES[j]
                if what == "max":
                    last = nc.tensor.transpose(m_ps[:, 0:P], amax[:, :], ident32[:, :])
                elif what == "spread":
                    last = mm(m_ps[:, 0:4], ones32[:, :], top_diag[:, :], start=True, stop=True)
                elif what in ("wqk", "wvo"):
                    for b in range(4):
                        last = nc.tensor.transpose(m_ps[:, b * P:(b + 1) * P],
                                                   w_raw[:, 2 * (what == "wvo") + b // 2, (b % 2) * P:(b % 2 + 1) * P],
                                                   ident32[:, :])
                elif what in "kq":
                    m = "qk".index(what)
                    n = 0
                    for wt, xt in ((w_hi, xt_hi), (w_hi, xt_lo), (w_lo, xt_hi)):
                        for kd in range(KD):
                            last = mm(m_ps[:, :], wt[:, m, kd, :], xt[:, kd, c * BANK:(c + 1) * BANK],
                                      start=(n == 0), stop=(n == 3 * KD - 1))
                            n += 1
                else:
                    for b in range(TPC):
                        t = c * TPC + b
                        n = 0
                        for xt, wt in ((xt_hi, w_hi), (xt_hi, w_lo), (xt_lo, w_hi)):
                            for kd in range(KD):
                                last = mm(m_ps[:, b * P:(b + 1) * P], xt[:, kd, t * P:(t + 1) * P], wt[:, 2, kd, :],
                                          start=(n == 0), stop=(n == 3 * KD - 1))
                                n += 1
                last.then_inc(piece_full, 1)
                return last

            pe.wait_ge(consts_ready, 6)
            pe.wait_ge(amax_ready, 1)
            for j in range(W_PIECES):
                if j > 0:
                    pe.wait_ge(piece_hi_done, j)
                    pe.wait_ge(piece_lo_done, j)
                piece(j)
            pe.wait_ge(piece_hi_done, W_PIECES)
            pe.wait_ge(piece_lo_done, W_PIECES)

            def turn_x(c):
                pe.wait_ge(xn_ready, (c + 1) * TPC)
                for kd in range(KD):
                    if c > 0:
                        pe.wait_ge(xt_hi_done, KD * (c - 1) + kd + 1)
                        pe.wait_ge(xt_lo_done, KD * (c - 1) + kd + 1)
                    for t in range(TPC):
                        last = nc.tensor.transpose(t_f32[kd][:, t * P:(t + 1) * P],
                                                   xn[:, c * TPC + t, kd * P:(kd + 1) * P], ident32[:, :])
                    last.then_inc(xt_full, 1)

            turn_x(0)
            for j in range(W_PIECES, KQ_PIECES):
                c = PIECES[j][1]
                if PIECES[j][0] == "k":
                    if c + 1 < NC:
                        turn_x(c + 1)
                    pe.wait_ge(xt_hi_done, KD * (c + 1))
                    pe.wait_ge(xt_lo_done, KD * (c + 1))
                if j >= W_PIECES + 4:
                    pe.wait_ge(piece_hi_done, j - 3)
                    pe.wait_ge(piece_lo_done, j - 3)
                piece(j, s_ps[:, j % 4, :])
            for j in range(KQ_PIECES, NP):
                piece(j, head0_bank(j))

            def transposes(it, k, g):
                if not exists(it, k) or g >= NG[tile_of(k)]:
                    return
                pp, t = par(k), tile_of(k)
                for src, dst, ready, full, read in ((p_hi, t_hi, p_hi_ready, t_hi_full, pt_hi_ready),
                                                    (p_lo, t_lo, p_lo_ready, t_lo_full, pt_lo_ready)):
                    pe.wait_ge(ready, tiles(it, k))
                    before = groups(it, k) + (g - NG[t])
                    if not (isinstance(before, int) and before <= 0):
                        pe.wait_ge(read, before)
                    for b in GROUPS[t][g]:
                        last = nc.tensor.transpose(dst[:, b - GROUPS[t][g][0], :], src[:, pp, b * P:(b + 1) * P], ident16[:, :])
                    last.then_inc(full, 1)

            def values(it, k, part):
                if not exists(it, k):
                    return
                hp, pp, n = hpar(k), par(k), tile_of(k) + 1
                if part == 0:
                    pe.wait_ge(pt_hi_ready, groups(it, k))
                    pe.wait_ge(pt_lo_ready, groups(it, k))
                    if k % QT == 0:
                        pe.wait_ge(piece_hi_done, pieces(it, k - QT, NP - 1))
                        pe.wait_ge(piece_lo_done, pieces(it, k - QT, NP - 1))
                    if exists(it, k - 1):
                        pe.wait_ge(z_hi_ready, tiles(it, k - 1))
                        pe.wait_ge(z_lo_ready, tiles(it, k - 1))
                for b in (range(0, n // 2), range(n // 2, n))[part]:
                    mm(z_ps[:, 0:P], v_hi[:, hp, b, :], pt_hi[:, pp, b, :], start=(b == 0), stop=False)
                    mm(z_ps[:, 0:P], v_hi[:, hp, b, :], pt_lo[:, pp, b, :], start=False, stop=False)
                    last = mm(z_ps[:, 0:P], v_lo[:, hp, b, :], pt_hi[:, pp, b, :], start=False, stop=(b == n - 1))
                if part == 1:
                    last.then_inc(pv_done, 1)

            def ffn_step(i):
                if i < QT:
                    if i == 0:
                        pe.wait_ge(exp_done, PAIRS * SLOTS)
                        pe.wait_ge(f_sum_step, R - 1)
                    pe.wait_ge(xn_ready, QT + i + 1)
                    if i >= 2:
                        pe.wait_ge(x2t_ready, i - 1)
                    for kd in range(KD):
                        last = nc.tensor.transpose(s_ps[:, i % 2, kd * P:(kd + 1) * P],
                                                   xn2[:, ORDER[i], kd * P:(kd + 1) * P], ident32[:, :])
                    last.then_inc(x2_full, 1)
                if i >= 1:
                    i -= 1
                    pe.wait_ge(x2t_ready, i + 1)
                    if i >= 2:
                        pe.wait_ge(res_ready, i - 1)
                    for kd in range(KD):
                        last = mm(s_ps[:, 2 + i % 2, 0:D], x2t[:, i % 2, kd, :], f_sum[:, kd, :],
                                  start=(kd == 0), stop=(kd == KD - 1))
                    last.then_inc(ffn_full, 1)

            def slot(it, k):
                if exists(it, k):
                    t, hp = tile_of(k), hpar(k)
                    if k % QT == 0:
                        pe.wait_ge(piece_hi_done, pieces(it, k - QT, KQ_PIECES - 1))
                        pe.wait_ge(piece_lo_done, pieces(it, k - QT, KQ_PIECES - 1))
                    f = s_free_after(k)
                    if exists(it, f):
                        pe.wait_ge(exp_done, tiles(it, f))
                    nb = -(-(t + 1) // TPC)
                    b0 = S_BASE[k % QT]
                    cols = (t + 1) * P
                    tq = slice(t * P, (t + 1) * P)
                    for b in range(nb):
                        w = min(BANK, cols - b * BANK)
                        ks = slice(b * BANK, b * BANK + w)
                        mm(s_ps[:, b0 + b, 0:w], q_hi[:, hp, tq], k_hi[:, hp, ks], start=True, stop=False)
                        mm(s_ps[:, b0 + b, 0:w], q_hi[:, hp, tq], k_lo[:, hp, ks], start=False, stop=False)
                        last = mm(s_ps[:, b0 + b, 0:w], q_lo[:, hp, tq], k_hi[:, hp, ks], start=False, stop=(b < nb - 1))
                        if b == 1 and nb > 2:
                            last.then_inc(scores_half, 1)
                    w = cols - (nb - 1) * BANK
                    mm(s_ps[:, b0 + nb - 1, w - P:w], ident_b[:, :], mask_b[:, :],
                       start=False, stop=True).then_inc(scores_done, 1)
                transposes(it, k - LAG_T, 0)
                values(it, k - LAG_PV, 0)
                ko = k - LAG_OUT
                if exists(it, ko):
                    pe.wait_ge(z_hi_ready, tiles(it, ko))
                    pe.wait_ge(z_lo_ready, tiles(it, ko))
                    pe.wait_ge(piece_hi_done, pieces_before(it, k))
                    pe.wait_ge(piece_lo_done, pieces_before(it, k))
                    zp, hp = par(ko), hpar(ko)
                    mm(m_ps[:, 0:D], z_hi[:, zp, :], wo_hi[:, hp, :], start=True, stop=False)
                    mm(m_ps[:, 0:D], z_hi[:, zp, :], wo_lo[:, hp, :], start=False, stop=False)
                    mm(m_ps[:, 0:D], z_lo[:, zp, :], wo_hi[:, hp, :], start=False, stop=True).then_inc(out_full, 1)
                values(it, k - LAG_PV, 1)
                transposes(it, k - LAG_T, 1)
                j = piece_of(it, k)
                if j is not None:
                    if exists(it, ko):
                        pe.wait_ge(acc_added, tiles(it, ko))
                    pe.wait_ge(piece_hi_done, pieces_before(it, k))
                    pe.wait_ge(piece_lo_done, pieces_before(it, k))
                    if j == 0:
                        pe.wait_ge(amax_ready, it * 2 + (k // QT + 2))
                    piece(j)
                for i in ffn_steps(it, k):
                    ffn_step(i)

            run_slots(pe, slot)
            for i in range(LN2_PARTS[1][0], QT + 1):
                ffn_step(i)

        @block.scalar
        def _(act):
            def piece_hi(j, hp, full, m_ps=m_ps):
                act.wait_ge(piece_full, full)
                what, c = PIECES[j]
                if what == "max":
                    nc.scalar.copy(amax_t[:, :], m_ps[:, 0:P]).then_inc(piece_hi_done, 1)
                elif what == "spread":
                    nc.scalar.copy(gmax[:, :], m_ps[:, 0:4]).then_inc(piece_hi_done, 1)
                elif what == "wqk":
                    nc.scalar.mul(w_hi[:, 0, :, :], m_ps[:, 0:D], w_scale[:, 0:1])
                    nc.scalar.mul(w_hi[:, 1, :, :], m_ps[:, D:2 * D], w_scale[:, 1:2]).then_inc(piece_hi_done, 1)
                elif what == "wvo":
                    nc.scalar.mul(w_hi[:, 2, :, :], m_ps[:, 0:D], w_scale[:, 2:3])
                    nc.scalar.mul(wo_hi[:, hp, :], m_ps[:, D:2 * D], w_scale[:, 3:4]).then_inc(piece_hi_done, 1)
                else:
                    if what == "v":
                        dst = v_hi[:, hp, c * TPC:(c + 1) * TPC, :]
                    else:
                        dst = (k_hi if what == "k" else q_hi)[:, hp, c * BANK:(c + 1) * BANK]
                    nc.scalar.mul(dst, m_ps[:, :], QKV_DOWN).then_inc(piece_hi_done, 1)

            def xt_hi_part(c):
                for kd in range(KD):
                    act.wait_ge(xt_full, KD * c + kd + 1)
                    nc.scalar.copy(xt_hi[:, kd, c * BANK:(c + 1) * BANK], t_f32[kd]).then_inc(xt_hi_done, 1)

            for j in range(W_PIECES):
                piece_hi(j, 0, j + 1)
            act.wait_ge(ln_step, 1)
            nc.scalar.activation(std[:, :], var_eps[:, :], ACT.Sqrt).then_inc(std_ready, 1)
            xt_hi_part(0)
            for j in range(W_PIECES, NP):
                if PIECES[j][0] == "k" and PIECES[j][1] + 1 < NC:
                    xt_hi_part(PIECES[j][1] + 1)
                piece_hi(j, 0, j + 1, head0_bank(j))

            def second_std(n):
                a, b = LN2_PARTS[n]
                act.wait_ge(ln_step, (n + 1) * LN_STEPS + 1)
                nc.scalar.activation(std[:, a:b], var_eps[:, a:b], ACT.Sqrt).then_inc(std_ready, 1)

            def x2t_copy(i):
                act.wait_ge(x2_full, i + 1)
                if i >= 2:
                    act.wait_ge(ffn_full, i - 1)
                nc.scalar.copy(x2t[:, i % 2, :, :], s_ps[:, i % 2, 0:D]).then_inc(x2t_ready, 1)

            def slot(it, k):
                if k == SLOTS and isinstance(it, int):
                    second_std(0)
                kt = k - LAG_T
                if exists(it, kt):
                    pp, n = par(kt), len(GROUPS[tile_of(kt)][0])
                    for src, dst, full, read in ((t_hi, pt_hi, t_hi_full, pt_hi_ready), (t_lo, pt_lo, t_lo_full, pt_lo_ready)):
                        act.wait_ge(full, groups(it, kt) + (1 - NG[tile_of(kt)]))
                        nc.scalar.copy(dst[:, pp, 0:n, :], src[:, 0:n, :]).then_inc(read, 1)
                if exists(it, k):
                    w = (tile_of(k) + 1) * P
                    b0, pp = S_BASE[k % QT], par(k)
                    act.wait_ge(bias_ready, tiles(it, k))
                    if exists(it, k - 2):
                        act.wait_ge(p_lo_ready, tiles(it, k - 2))
                    nc.scalar.activation(prob[:, pp, 0:w], s_ps[:, :, :].rearrange("p b n -> p (b n)")[:, b0 * BANK:b0 * BANK + w],
                                         ACT.Exp, bias=exp_bias[:, pp:pp + 1], scale=c_score[:, hpar(k):hpar(k) + 1],
                                         accum_out=row_sum[:, pp:pp + 1]).then_inc(exp_done, 1)
                j = piece_of(it, k)
                if j is not None:
                    piece_hi(j, 1 - hpar(k), pieces(it, k, j))
                for i in ffn_steps(it, k):
                    x2t_copy(i)

            run_slots(act, slot)
            second_std(1)
            for i in range(LN2_PARTS[1][0], QT):
                x2t_copy(i)

        @block.vector
        def _(dve):
            v = nc.vector

            def row_stats(i, t, before):
                v.bn_stats(stats[:, i, :], acc[:, t, :]).then_inc(stats_done, 1)
                dve.wait_ge(stats_done, before + 1)
                v.bn_aggr(mean_var[:, i, :], stats[:, i, :]).then_inc(aggr_done, 1)

            def row_variances(a, b, columns):
                dve.wait_ge(aggr_done, columns)
                v.tensor_scalar(var_eps[:, a:b], mean_var[:, a:b, 1], LN_EPS, None, ALU.add).then_inc(ln_step, 1)

            def row_factors(call, a, b, scale):
                n = call * LN_STEPS
                dve.wait_ge(std_ready, call + 1)
                v.reciprocal(rstd0[:, a:b], std[:, a:b]).then_inc(ln_step, 1)
                dve.wait_ge(ln_step, n + 2)
                v.tensor_tensor(newton[:, a:b], rstd0[:, a:b], rstd0[:, a:b], ALU.mult).then_inc(ln_step, 1)
                dve.wait_ge(ln_step, n + 3)
                v.tensor_tensor(std[:, a:b], newton[:, a:b], var_eps[:, a:b], ALU.mult).then_inc(ln_step, 1)
                dve.wait_ge(ln_step, n + 4)
                v.tensor_scalar(newton[:, a:b], std[:, a:b], -0.5 * scale, 1.5 * scale, ALU.mult, ALU.add).then_inc(ln_step, 1)
                dve.wait_ge(ln_step, n + 5)
                v.tensor_tensor(rstd[:, a:b], newton[:, a:b], rstd0[:, a:b], ALU.mult).then_inc(ln_step, 1)
                dve.wait_ge(ln_step, n + 6)

            def normalise(xn, i, t):
                v.tensor_scalar(xn[:, t, :], acc[:, t, :], mean_var[:, i, 0:1], rstd[:, i:i + 1],
                                ALU.subtract, ALU.mult).then_inc(xn_ready, 1)

            def head_amax(count):
                dve.wait_ge(w_loaded, count * 64)
                v.tensor_reduce(amax[:, 0:4], w_raw[:, :, :], AX.X, ALU.max,
                                apply_absolute_value=True).then_inc(amax_ready, 1)

            def head_scales(count, hp):
                n = count * 3 - 3
                v.tensor_scalar(gclamp[:, :], gmax[:, :], 1e-30, None, ALU.max).then_inc(scale_step, 1)
                dve.wait_ge(scale_step, n + 1)
                v.tensor_scalar(pow2[:, :].bitcast(U32), gclamp[:, :].bitcast(U32), EXPONENT_BITS, None,
                                ALU.bitwise_and).then_inc(scale_step, 1)
                dve.wait_ge(scale_step, n + 2)
                v.tensor_scalar(w_inv[:, :], pow2[:, :], 1.0 / W_TOP, None, ALU.mult).then_inc(scale_step, 1)
                dve.wait_ge(scale_step, n + 3)
                v.scalar_tensor_tensor(c_score[:, hp:hp + 1], w_inv[:, 0:1],
                                       float(Dh) ** -0.5 / (X_SCALE * QKV_DOWN) ** 2, w_inv[:, 1:2],
                                       ALU.mult, ALU.mult)
                v.scalar_tensor_tensor(c_out[:, hp:hp + 1], w_inv[:, 2:3], 1.0 / (X_SCALE * QKV_DOWN), w_inv[:, 3:4],
                                       ALU.mult, ALU.mult)
                v.reciprocal(w_scale[:, :], w_inv[:, :]).then_inc(piece_lo_done, 1)

            def piece_lo(j, hp, done, count, m_ps=m_ps):
                dve.wait_ge(piece_hi_done, done)
                what, c = PIECES[j]
                if what == "max":
                    v.tensor_reduce(top[:, :], amax_t[:, :], AX.X, ALU.max).then_inc(top_ready, 1)
                    dve.wait_ge(top_ready, count)
                    v.tensor_scalar(top_diag[:, :], ident32[:, 0:4], top[:, 0:1], None, ALU.mult).then_inc(piece_lo_done, 1)
                    return
                if what == "spread":
                    head_scales(count, hp)
                    return
                if what in ("wqk", "wvo"):
                    for m in range(2):
                        i = 2 * (what == "wvo") + m
                        hi, lo = (wo_hi[:, hp, :], wo_lo[:, hp, :]) if i == 3 else (
                            w_hi[:, i, :, :].rearrange("p k h -> p (k h)"), w_lo[:, i, :, :].rearrange("p k h -> p (k h)"))
                        last = v.scalar_tensor_tensor(lo, m_ps[:, m * D:(m + 1) * D], w_scale[:, i:i + 1], hi,
                                                      ALU.mult, ALU.subtract)
                else:
                    if what == "v":
                        hi, lo = (a[:, hp, c * TPC:(c + 1) * TPC, :].rearrange("p t h -> p (t h)") for a in (v_hi, v_lo))
                    else:
                        hi, lo = (a[:, hp, c * BANK:(c + 1) * BANK] for a in ((k_hi, k_lo) if what == "k" else (q_hi, q_lo)))
                    last = v.scalar_tensor_tensor(lo, m_ps[:, :], QKV_DOWN, hi, ALU.mult, ALU.subtract)
                last.then_inc(piece_lo_done, 1)

            def xt_lo_part(c):
                for kd in range(KD):
                    dve.wait_ge(xt_hi_done, KD * c + kd + 1)
                    v.tensor_tensor(xt_lo[:, kd, c * BANK:(c + 1) * BANK], t_f32[kd],
                                    xt_hi[:, kd, c * BANK:(c + 1) * BANK], ALU.subtract).then_inc(xt_lo_done, 1)

            dve.wait_ge(consts_ready, 6)
            head_amax(1)
            for c in range(NC):
                dve.wait_ge(x_loaded[c], 16)
                for t in range(c * TPC, (c + 1) * TPC):
                    row_stats(t, t, t)
                piece_lo(c, 0, c + 1, 1)
            row_variances(0, QT, QT)
            row_factors(0, 0, QT, X_SCALE)
            for t in range(2 * TPC):
                normalise(xn, t, t)
            xt_lo_part(0)
            for j in range(W_PIECES, NP):
                what, c = PIECES[j]
                if what == "k" and c + 1 < NC:
                    for t in range((c + 2) * TPC, min((c + 3) * TPC, QT)):
                        normalise(xn, t, t)
                    xt_lo_part(c + 1)
                piece_lo(j, 0, j + 1, 1, head0_bank(j))
                if j == NP - 1:
                    head_amax(2)

            def max_steps(it, k, step):
                return it * (SLOTS + 2 * SPLIT_HEAD) + (k + 1 + (halves(0, k) if step == 2 or tile_of(k) < 2 * TPC else halves(0, k) - 1))

            def second_variances(n):
                a, b = LN2_PARTS[n]
                row_variances(a, b, QT + b)

            def second_rows(n, a, b):
                if a == LN2_PARTS[n][0]:
                    row_factors(1 + n, *LN2_PARTS[n], 1.0)
                    dve.wait_ge(f_sum_step, R - 1)
                for i in range(a, b):
                    normalise(xn2, i, ORDER[i])

            def result(i):
                dve.wait_ge(ffn_full, i + 1)
                dve.wait_ge(resid_ready, i + 1)
                v.scalar_tensor_tensor(res[:, ORDER[i], :], s_ps[:, 2 + i % 2, 0:D], float(R) ** -0.5,
                                       resid[:, ORDER[i], :], ALU.mult, ALU.add).then_inc(res_ready, 1)

            def slot(it, k):
                if exists(it, k):
                    w, pp, b0 = (tile_of(k) + 1) * P, par(k), S_BASE[k % QT]
                    s_flat = s_ps[:, :, :].rearrange("p b n -> p (b n)")[:, b0 * BANK:b0 * BANK + w]
                    split = 2 * BANK if w > 2 * BANK else 0
                    if split:
                        dve.wait_ge(scores_half, halves(it, k))
                        v.tensor_reduce(neg_max_half[:, pp:pp + 1], s_flat[:, 0:split], AX.X, ALU.max, negate=True)
                    dve.wait_ge(scores_done, tiles(it, k))
                    v.tensor_reduce(neg_max[:, pp:pp + 1], s_flat[:, split:w], AX.X, ALU.max, negate=True).then_inc(max_done, 1)
                    dve.wait_ge(max_done, max_steps(it, k, 1))
                    if split:
                        v.tensor_tensor(neg_max[:, pp:pp + 1], neg_max[:, pp:pp + 1], neg_max_half[:, pp:pp + 1],
                                        ALU.min).then_inc(max_done, 1)
                        dve.wait_ge(max_done, max_steps(it, k, 2))
                    v.tensor_scalar(exp_bias[:, pp:pp + 1], neg_max[:, pp:pp + 1], c_score[:, hpar(k):hpar(k) + 1],
                                    float(np.log(P_SCALE)), ALU.mult, ALU.add).then_inc(bias_ready, 1)
                kh = k - LAG_HI
                if exists(it, kh):
                    w, pp = (tile_of(kh) + 1) * P, par(kh)
                    dve.wait_ge(exp_done, tiles(it, kh))
                    v.tensor_copy(p_hi[:, pp, 0:w], prob[:, pp, 0:w]).then_inc(p_hi_ready, 1)
                ko = k - LAG_OUT
                if exists(it, ko):
                    dve.wait_ge(out_full, tiles(it, ko))
                    dve.wait_ge(out_scale_ready, tiles(it, ko))
                    t = tile_of(ko)
                    v.scalar_tensor_tensor(acc[:, t, :], m_ps[:, 0:D], out_scale[:, ko % 4:ko % 4 + 1], acc[:, t, :],
                                           ALU.mult, ALU.add).then_inc(acc_added, 1)
                    if isinstance(it, int) and it * SLOTS + ko >= (H - 1) * QT:
                        dve.wait_ge(acc_added, tiles(it, ko))
                        row_stats(ko % QT, t, QT + ko % QT)
                if exists(it, kh):
                    pp, hp = par(kh), hpar(kh)
                    v.reciprocal(row_rec[:, pp:pp + 1], row_sum[:, pp:pp + 1]).then_inc(rec_done, 1)
                    dve.wait_ge(rec_done, tiles(it, kh))
                    v.scalar_tensor_tensor(out_scale[:, kh % 4:kh % 4 + 1], row_rec[:, pp:pp + 1], 1.0 / z_down(tile_of(kh)),
                                           c_out[:, hp:hp + 1], ALU.mult, ALU.mult).then_inc(out_scale_ready, 1)
                kv = k - LAG_PV
                if exists(it, kv):
                    zp, down = par(kv), z_down(tile_of(kv))
                    dve.wait_ge(pv_done, tiles(it, kv))
                    v.tensor_scalar(z_hi[:, zp, :], z_ps[:, 0:P], down, None, ALU.mult).then_inc(z_hi_ready, 1)
                    dve.wait_ge(z_hi_ready, tiles(it, kv))
                    v.scalar_tensor_tensor(z_lo[:, zp, :], z_ps[:, 0:P], down, z_hi[:, zp, :],
                                           ALU.mult, ALU.subtract).then_inc(z_lo_ready, 1)
                kt = k - LAG_T
                if exists(it, kt):
                    pp, t = par(kt), tile_of(kt)
                    for g in range(1, NG[t]):
                        b, n = GROUPS[t][g][0], len(GROUPS[t][g])
                        for src, dst, full, read in ((t_hi, pt_hi, t_hi_full, pt_hi_ready), (t_lo, pt_lo, t_lo_full, pt_lo_ready)):
                            dve.wait_ge(full, groups(it, kt) + (g + 1 - NG[t]))
                            v.tensor_copy(dst[:, pp, b:b + n, :], src[:, 0:n, :]).then_inc(read, 1)
                j = piece_of(it, k)
                if j is not None:
                    piece_lo(j, 1 - hpar(k), pieces(it, k, j), it * 2 + (k // QT + 2))
                if k % QT == QT - 2 and exists(it, k) and not (isinstance(it, int) and 2 * it + k // QT + 2 >= H):
                    head_amax(it * 2 + (k // QT + 3))
                if isinstance(it, int) and it == PAIRS - 1:
                    half = LN2_PARTS[0][1] // 2
                    if k == SLOTS - 1:
                        second_variances(0)
                    if k == SLOTS:
                        second_rows(0, 0, half)
                    if k == SLOTS + 1:
                        second_rows(0, half, 2 * half)
                    for i in ffn_steps(it, k):
                        if i > 0:
                            result(i - 1)

            run_slots(dve, slot)

            second_variances(1)
            second_rows(1, LN2_PARTS[1][0], QT)
            for i in range(LN2_PARTS[1][0], QT + 1):
                result(i - 1)


_INS = ["L0_attn_x", "L0_attn_W_K", "L0_attn_W_Q", "L0_attn_W_V", "L0_attn_W_O", "L0_ffn_factors", "L0_ffn_bias"]


def kernel(**inputs):
    from concourse.bacc import Bacc
    from concourse.bass_utils import run_bass_kernel_spmd

    nc = Bacc("TRN2", target_bir_lowering=False, num_devices=1)
    arrays, args = {}, []
    for name in _INS:
        a = np.ascontiguousarray(inputs[name])
        arrays[f"in_{name}"] = a
        args.append(nc.dram_tensor(f"in_{name}", a.shape, mybir.dt.from_np(a.dtype), kind="ExternalInput").ap())
    out = nc.dram_tensor("out_x", inputs["L0_attn_x"].shape, F32, kind="ExternalOutput").ap()
    preln_attention_ffn(nc, *args, out)
    r = run_bass_kernel_spmd(nc, [arrays], core_ids=[0])
    return r.results[0]["out_x"]
```

```python
from contextlib import ExitStack

import numpy as np

import concourse.bass as bass
from concourse import mybir

ALU = mybir.AluOpType
ACT = mybir.ActivationFunctionType
AX = mybir.AxisListType
F32 = mybir.dt.float32
F16 = mybir.dt.float16
BF16 = mybir.dt.bfloat16
U32 = mybir.dt.uint32
WARM_UP = 24

P = 128
BANK = 512
LN_EPS = 1e-5

X_SCALE = 2.0 ** 11
W_TOP = 2.0 ** 13
QKV_DOWN = 2.0 ** -18
P_SCALE = 2.0 ** 15
EXPONENT_BITS = 0x7F800000


def preln_attention_ffn(nc, x, w_k, w_q, w_v, w_o, factors, bias, out):
    S, D = x.shape[1], x.shape[2]
    H, Dh = w_k.shape[0], w_k.shape[1]
    R = factors.shape[0]
    QT = S // P
    KD = D // P
    NC = S // BANK
    TPC = BANK // P
    PAIRS = H // 2
    assert Dh == P and D == 2 * P and QT == 16 and H % 2 == 0 and NC == 4

    LAG_HI, LAG_PV, LAG_OUT = 1, 4, 5
    PRO = LAG_OUT
    SLOTS = 2 * QT
    LN2_PART = 4
    LN2_LAG = LAG_OUT + LN2_PART - 1
    FFN_LAG = LN2_LAG + 2
    FFN_IN_SLOTS = QT + LAG_OUT - FFN_LAG
    ORDER = [t for i in (6, 7, 0, 1, 2, 3, 5, 4) for t in (QT - 1 - i, i)]

    PIECES = [("max", 0), ("spread", 0), ("wqk", 0), ("k", 0), ("q", 0), ("k", 1), ("wvo", 0), ("q", 1)]
    for c in range(2, NC):
        PIECES += [("k", c), ("q", c)]
    PIECES += [("v", c) for c in range(NC)]
    NP = len(PIECES)
    KQ_PIECES = NP - NC
    assert NP == QT
    WQK, WVO = (PIECES.index((w, 0)) for w in ("wqk", "wvo"))
    PT = 4

    def z_down(t):
        return 2.0 ** -(15 + int(np.ceil(np.log2((t + 1) * P))))

    def tile_of(k):
        return ORDER[k % QT]

    def par(k):
        return k % 2

    def hpar(k):
        return (k // QT) % 2

    def tiles(it, k):
        return it * SLOTS + (k + 1)

    SPLIT_HEAD = sum(t >= 2 * TPC for t in ORDER)

    def halves(it, k):
        return it * (2 * SPLIT_HEAD) + ((k // QT) * SPLIT_HEAD + sum(ORDER[i] >= 2 * TPC for i in range(k % QT + 1)))

    def transposed(it, k):
        return it * (16 * SLOTS // PT) + 16 * (k // PT + 1)

    def pieces(it, k, j):
        return it * (2 * NP) + (NP * (k // QT + 1) + j + 1)

    def pieces_before(it, k):
        if isinstance(it, int) and 2 * it + k // QT + 1 >= H:
            return NP * H
        return it * (2 * NP) + (NP * (k // QT + 1) + k % QT)

    def piece_of(it, k):
        return None if isinstance(it, int) and 2 * it + k // QT + 1 >= H else k % QT

    def exists(it, k):
        return not isinstance(it, int) or (k >= 0 and it * SLOTS + k < PAIRS * SLOTS)

    def is_slot(it, k, n):
        return isinstance(it, int) and it == 0 and k == n

    def ffn_step_of(it, k):
        i = k - (SLOTS - QT) - FFN_LAG
        return i if isinstance(it, int) and it == PAIRS - 1 and 0 <= i < FFN_IN_SLOTS else None

    def ln2_position(it, k):
        i = k - (SLOTS - QT) - LN2_LAG
        return i if isinstance(it, int) and it == PAIRS - 1 and 0 <= i < QT - LN2_PART else None

    def run_slots(eng, slot):
        for k in range(PRO):
            slot(0, k)
        with eng.Fori(0, PAIRS - 1) as it:
            for k in range(PRO, PRO + SLOTS):
                slot(it, k)
        for k in range(PRO, SLOTS + LAG_OUT):
            slot(PAIRS - 1, k)

    S_BANKS = NC + 1
    S_BASE = [{1: 4, 2: 3, 3: 0, 4: 0}[-(-(t + 1) // TPC)] for t in ORDER]

    def s_banks(k):
        b = S_BASE[k % QT]
        return set(range(b, b + -(-(tile_of(k) + 1) // TPC)))

    def s_free_after(k, bank):
        for d in range(1, QT):
            if bank in s_banks(k - d + SLOTS):
                return k - d

    with ExitStack() as ctx:
        def sb(name, shape, dt):
            return ctx.enter_context(nc.sbuf_tensor(name, shape, dt))

        def ps(name, shape, dt):
            return ctx.enter_context(nc.psum_tensor(name, shape, dt))

        def sem(name):
            return ctx.enter_context(nc.semaphore(name))

        acc = sb("acc", [P, QT, D], F32)
        xt_hi = sb("xt_hi", [P, KD, S], F16)
        xt_lo = sb("xt_lo", [P, KD, S], F16)
        w_raw = sb("w_raw", [P, 4, D], F32)
        w_hi = sb("w_hi", [P, 3, KD, P], F16)
        w_lo = sb("w_lo", [P, 3, KD, P], F16)
        wo_hi = sb("wo_hi", [P, 2, D], F16)
        wo_lo = sb("wo_lo", [P, 2, D], F16)
        k_hi = sb("k_hi", [P, 2, S], F16)
        k_lo = sb("k_lo", [P, 2, S], F16)
        q_hi = sb("q_hi", [P, 2, S], F16)
        q_lo = sb("q_lo", [P, 2, S], F16)
        v_hi = sb("v_hi", [P, 2, QT, P], F16)
        v_lo = sb("v_lo", [P, 2, QT, P], F16)
        prob = sb("prob", [P, 2, S], F32)
        p_hi = sb("p_hi", [P, 2, S], F16)
        p_lo = sb("p_lo", [P, 2, S], F16)
        pt_hi = sb("pt_hi", [P, PT, QT, P], F16)
        pt_lo = sb("pt_lo", [P, PT, QT, P], F16)
        z_hi = sb("z_hi", [P, 2, P], F16)
        z_lo = sb("z_lo", [P, 2, P], F16)
        ident32 = sb("ident32", [P, P], F32)
        ident_b = sb("ident_b", [P, P], BF16)
        mask_b = sb("mask_b", [P, P], BF16)
        ones32 = sb("ones32", [P, P], F32)
        amax = sb("amax", [P, P], F32)
        amax_t = sb("amax_t", [P, P], F32)
        top = sb("top", [P, 1], F32)
        top_diag = sb("top_diag", [P, 4], F32)
        gmax = sb("gmax", [P, 4], F32)
        gclamp = sb("gclamp", [P, 4], F32)
        pow2 = sb("pow2", [P, 4], F32)
        w_inv = sb("w_inv", [P, 4], F32)
        w_scale = sb("w_scale", [P, 4], F32)
        c_score = sb("c_score", [P, 2], F32)
        c_out = sb("c_out", [P, 2], F32)
        neg_max = sb("neg_max", [P, 2], F32)
        neg_max_half = sb("neg_max_half", [P, 2], F32)
        exp_bias = sb("exp_bias", [P, 2], F32)
        row_sum = sb("row_sum", [P, 2], F32)
        row_rec = sb("row_rec", [P, 2], F32)
        out_scale = sb("out_scale", [P, 8], F32)
        stats = sb("stats", [P, QT, 6], F32)
        mean_var = sb("mean_var", [P, QT, 2], F32)
        var_eps = sb("var_eps", [P, QT], F32)
        std = sb("std", [P, QT], F32)
        rstd0 = sb("rstd0", [P, QT], F32)
        nr = sb("nr", [P, QT], F32)
        exp_warm = sb("exp_warm", [P, 1], F32)
        nr_var = sb("nr_var", [P, QT], F32)
        rstd = sb("rstd", [P, QT], F32)
        f_raw = sb("f_raw", [P, R, KD, D], F32)
        f_sum = sb("f_sum", [P, KD, D], F32)
        bias_row = sb("bias_row", [P, D], F32)
        x2t = sb("x2t", [P, 2, KD, P], F32)
        xn = prob[:, :, :].rearrange("p a (t d) -> p (a t) d", d=D)
        f_rows = f_raw[:, :, :, :].rearrange("p r k e -> p (r k) e")
        xn2 = f_rows
        res = f_rows

        s_ps = ps("s_ps", [P, S_BANKS, BANK], F32)
        z_ps = ps("z_ps", [P, BANK], F32)
        o_ps = ps("o_ps", [P, BANK], F32)
        m_ps = ps("m_ps", [P, BANK], F32)
        x_ps = [z_ps, o_ps]

        def head0_place(j):
            what, c = PIECES[j]
            if what in "kq":
                return (2 * c + (what == "q")) % 4
            return NC if what == "wvo" else "mzom"[c] if what == "v" else "m"

        def head0_bank(j):
            at = head0_place(j)
            return s_ps[:, at, :] if isinstance(at, int) else {"m": m_ps, "z": z_ps, "o": o_ps}[at][:, :]

        def head0_before(j):
            needs = WVO + 1 if PIECES[j][0] == "v" else WQK + 1 if PIECES[j][0] in "kq" else 0
            return max([needs] + [i + 1 for i in range(j) if head0_place(i) == head0_place(j)])

        def ffn_banks(i):
            if i < FFN_IN_SLOTS:
                return m_ps[:, 0:D], m_ps[:, D:2 * D]
            return s_ps[:, i % 2, 0:D], s_ps[:, 2 + i % 2, 0:D]

        CONSTS = 5
        x_loaded = [sem(f"x_loaded{c}") for c in range(NC)]
        w_loaded = sem("w_loaded")
        f_loaded = sem("f_loaded")
        consts_zero = sem("consts_zero")
        consts_ready = sem("consts_ready")
        stats_done = sem("stats_done")
        aggr_done = sem("aggr_done")
        var_ready = sem("var_ready")
        std_ready = sem("std_ready")
        rstd0_ready = sem("rstd0_ready")
        newton_step = sem("newton_step")
        xn_ready = sem("xn_ready")
        xt_full = sem("xt_full")
        xt_hi_done = sem("xt_hi_done")
        xt_lo_done = sem("xt_lo_done")
        amax_ready = sem("amax_ready")
        top_ready = sem("top_ready")
        scale_step = sem("scale_step")
        piece_full = sem("piece_full")
        piece_hi_done = sem("piece_hi_done")
        piece_lo_done = sem("piece_lo_done")
        scores_done = sem("scores_done")
        scores_half = sem("scores_half")
        max_done = sem("max_done")
        bias_ready = sem("bias_ready")
        exp_done = sem("exp_done")
        rec_done = sem("rec_done")
        out_scale_ready = sem("out_scale_ready")
        p_hi_ready = sem("p_hi_ready")
        p_lo_ready = sem("p_lo_ready")
        pt_hi_ready = [sem(f"pt_hi_ready{i}") for i in range(PT)]
        pt_lo_ready = [sem(f"pt_lo_ready{i}") for i in range(PT)]
        pv_done = sem("pv_done")
        z_hi_ready = sem("z_hi_ready")
        z_lo_ready = sem("z_lo_ready")
        out_full = sem("out_full")
        acc_added = sem("acc_added")
        f_sum_step = sem("f_sum_step")
        resid_ready = sem("resid_ready")
        x2_full = sem("x2_full")
        x2t_ready = sem("x2t_ready")
        ffn_full = sem("ffn_full")
        res_ready = sem("res_ready")
        stored = sem("stored")

        x_dram = x.rearrange("b (t p) d -> p (b t) d", p=P)
        out_dram = out.rearrange("b (t p) d -> p (b t) d", p=P)
        wo_dram = w_o.rearrange("(k p) (i h) -> p k i h", p=P, h=Dh)
        f_dram = factors.rearrange("r (k p) e -> p r k e", p=P)

        block = ctx.enter_context(nc.Block())

        def newton(engine, queue, call, a, b, scale):
            n = 4 * call
            queue.wait_ge(rstd0_ready, call + 1)
            engine.tensor_tensor(out=nr[:, a:b], in0=rstd0[:, a:b], in1=rstd0[:, a:b], op=ALU.mult).then_inc(newton_step, 1)
            queue.wait_ge(newton_step, n + 1)
            engine.tensor_tensor(out=nr_var[:, a:b], in0=nr[:, a:b], in1=var_eps[:, a:b], op=ALU.mult).then_inc(newton_step, 1)
            queue.wait_ge(newton_step, n + 2)
            engine.tensor_scalar(out=nr[:, a:b], in0=nr_var[:, a:b], scalar1=-0.5 * scale, scalar2=1.5 * scale,
                                 op0=ALU.mult, op1=ALU.add).then_inc(newton_step, 1)
            queue.wait_ge(newton_step, n + 3)
            engine.tensor_tensor(out=rstd[:, a:b], in0=nr[:, a:b], in1=rstd0[:, a:b], op=ALU.mult).then_inc(newton_step, 1)

        def normalise(engine, xn, i, t):
            engine.tensor_scalar(out=xn[:, t, :], in0=acc[:, t, :], scalar1=mean_var[:, i, 0:1], scalar2=rstd[:, i:i + 1],
                                 op0=ALU.subtract, op1=ALU.mult).then_inc(xn_ready, 1)

        @block.sync
        def _(sp):
            def load_weights(head):
                for j, w in enumerate((w_q, w_k, w_v)):
                    sp.dma_start(w_raw[:, j, :], w[bass.ds(head, 1)].rearrange("i h d -> h (i d)")).then_inc(w_loaded, 16)
                sp.dma_start(w_raw[:, 3, :].rearrange("p (k h) -> p k h", k=KD),
                             wo_dram[:, :, bass.ds(head, 1), :].rearrange("p k i h -> p k (i h)")).then_inc(w_loaded, 16)

            for c in range(NC):
                if c == 1:
                    load_weights(0)
                sp.dma_start(acc[:, c * TPC:(c + 1) * TPC, :], x_dram[:, c * TPC:(c + 1) * TPC, :]).then_inc(x_loaded[c], 16)
            sp.dma_start(f_raw[:, :, :, :].rearrange("p r k e -> p (r k) e"),
                         f_dram.rearrange("p r k e -> p (r k) e")).then_inc(f_loaded, 16)
            sp.dma_start(bias_row[:, :], bias.rearrange("(a d) -> a d", a=1).broadcast_to([P, D])).then_inc(f_loaded, 16)
            sp.wait_ge(piece_full, WVO + 1)
            load_weights(1)

            def slot(it, k):
                kh = k - LAG_HI
                if exists(it, kh):
                    pp, pt, n = par(kh), kh % PT, tile_of(kh) + 1
                    made, used = (tiles(it, i) if isinstance(it, int) else sp.to_reg(tiles(it, i))
                                  for i in (kh, kh - PT))
                    for src, dst, ready, read in ((p_hi, pt_hi, p_hi_ready, pt_hi_ready), (p_lo, pt_lo, p_lo_ready, pt_lo_ready)):
                        sp.wait_ge(consts_ready, CONSTS)
                        sp.wait_ge(ready, made)
                        if exists(it, kh - PT):
                            sp.wait_ge(pv_done, used)
                        sp.dma_start_transpose(dst[:, pt, 0:n, :], src[:, pp, 0:n * P]).then_inc(read[pt], 16)
                if k % QT == WVO + 2 and k < SLOTS and not (isinstance(it, int) and 2 * it + k // QT + 2 >= H):
                    sp.wait_ge(piece_full, pieces(it, k, WVO))
                    load_weights(it * 2 + (k // QT + 2))

            run_slots(sp, slot)
            for i, t in enumerate(ORDER):
                sp.wait_ge(res_ready, i + 1)
                sp.dma_start(out_dram[:, t, :], res[:, t, :]).then_inc(stored, 16)
            sp.wait_ge(stored, 16 * QT)

        @block.gpsimd
        def _(pool):
            for m in (ident32, ident_b, mask_b):
                nc.gpsimd.memset(m[:, :], 0.0).then_inc(consts_zero, 1)
            nc.gpsimd.memset(ones32[:, :], 1.0).then_inc(consts_ready, 1)
            nc.gpsimd.memset(amax[:, :], 0.0).then_inc(consts_ready, 1)
            pool.wait_ge(consts_zero, 3)
            for m in (ident32, ident_b):
                nc.gpsimd.affine_select(out=m[:, :], in_=m[:, :], compare_op=ALU.not_equal, fill=1.0, base=0,
                                        pattern=[[-1, P]], channel_multiplier=1).then_inc(consts_ready, 1)
            nc.gpsimd.affine_select(out=mask_b[:, :], in_=mask_b[:, :], compare_op=ALU.is_ge, fill=-3e38, base=0,
                                    pattern=[[-1, P]], channel_multiplier=1).then_inc(consts_ready, 1)

            for c in range(NC):
                newton(nc.gpsimd, pool, c, c * TPC, (c + 1) * TPC, X_SCALE)

            pool.wait_ge(f_loaded, 32)
            for r in range(1, R):
                if r > 1:
                    pool.wait_ge(f_sum_step, r - 1)
                nc.gpsimd.tensor_tensor(out=f_sum[:, :, :], in0=f_raw[:, 0, :, :] if r == 1 else f_sum[:, :, :],
                                        in1=f_raw[:, r, :, :], op=ALU.add).then_inc(f_sum_step, 1)

            def slot(it, k):
                if exists(it, k):
                    w, pp = (tile_of(k) + 1) * P, par(k)
                    if exists(it, k - 2):
                        pool.wait_ge(pt_lo_ready[(k - 2) % PT], transposed(it, k - 2))
                    pool.wait_ge(p_hi_ready, tiles(it, k))
                    nc.gpsimd.tensor_tensor(out=p_lo[:, pp, 0:w], in0=prob[:, pp, 0:w], in1=p_hi[:, pp, 0:w],
                                            op=ALU.subtract).then_inc(p_lo_ready, 1)
                if isinstance(it, int) and it == PAIRS - 1:
                    residual(k - (SLOTS - QT) - LN2_LAG - 1)

            def residual(i):
                if 0 <= i < QT:
                    pool.wait_ge(xn_ready, QT + i + 1)
                    nc.gpsimd.tensor_tensor(out=acc[:, ORDER[i], :], in0=acc[:, ORDER[i], :], in1=bias_row[:, :],
                                            op=ALU.add).then_inc(resid_ready, 1)

            run_slots(pool, slot)
            for i in range(QT + LAG_OUT - LN2_LAG - 1, QT):
                residual(i)

        @block.tensor
        def _(pe):
            mm = nc.tensor.matmul

            def piece(j, m_ps=m_ps[:, :]):
                what, c = PIECES[j]
                if what == "max":
                    last = nc.tensor.transpose(m_ps[:, 0:P], amax[:, :], ident32[:, :])
                elif what == "spread":
                    last = mm(m_ps[:, 0:4], ones32[:, :], top_diag[:, :], start=True, stop=True)
                elif what in ("wqk", "wvo"):
                    for b in range(4):
                        last = nc.tensor.transpose(m_ps[:, b * P:(b + 1) * P],
                                                   w_raw[:, 2 * (what == "wvo") + b // 2, (b % 2) * P:(b % 2 + 1) * P],
                                                   ident32[:, :])
                elif what in "kq":
                    m = "qk".index(what)
                    n = 0
                    for wt, xt in ((w_hi, xt_hi), (w_hi, xt_lo), (w_lo, xt_hi)):
                        for kd in range(KD):
                            last = mm(m_ps[:, :], wt[:, m, kd, :], xt[:, kd, c * BANK:(c + 1) * BANK],
                                      start=(n == 0), stop=(n == 3 * KD - 1))
                            n += 1
                else:
                    for b in range(TPC):
                        t = c * TPC + b
                        n = 0
                        for xt, wt in ((xt_hi, w_hi), (xt_hi, w_lo), (xt_lo, w_hi)):
                            for kd in range(KD):
                                last = mm(m_ps[:, b * P:(b + 1) * P], xt[:, kd, t * P:(t + 1) * P], wt[:, 2, kd, :],
                                          start=(n == 0), stop=(n == 3 * KD - 1))
                                n += 1
                last.then_inc(piece_full, 1)
                return last

            def turn_x(c):
                pe.wait_ge(xn_ready, (c + 1) * TPC)
                for kd in range(KD):
                    if c > 0:
                        pe.wait_ge(xt_hi_done, KD * (c - 1) + kd + 1)
                        pe.wait_ge(xt_lo_done, KD * (c - 1) + kd + 1)
                    for t in range(TPC):
                        last = nc.tensor.transpose(x_ps[kd][:, t * P:(t + 1) * P],
                                                   xn[:, c * TPC + t, kd * P:(kd + 1) * P], ident32[:, :])
                    last.then_inc(xt_full, 1)

            pe.wait_ge(consts_ready, CONSTS)
            for r in range(WARM_UP):
                nc.tensor.transpose(s_ps[:, 3, 0:P], ident32[:, :], ident32[:, :])

            def head0_piece(j):
                what, c = PIECES[j]
                if what in "kq":
                    pe.wait_ge(xt_hi_done, KD * (c + 1))
                    pe.wait_ge(xt_lo_done, KD * (c + 1))
                if head0_before(j):
                    pe.wait_ge(piece_hi_done, head0_before(j))
                    pe.wait_ge(piece_lo_done, head0_before(j))
                piece(j, head0_bank(j))

            pe.wait_ge(amax_ready, 1)
            head0_piece(0)
            head0_piece(1)
            head0_piece(2)
            turn_x(0)
            head0_piece(3)
            turn_x(1)
            head0_piece(4)
            head0_piece(5)
            turn_x(2)
            head0_piece(6)
            head0_piece(7)
            head0_piece(8)
            turn_x(3)
            head0_piece(9)
            head0_piece(10)
            head0_piece(11)

            def head0_values():
                for j in range(KQ_PIECES, NP):
                    head0_piece(j)

            def values(it, k, part):
                if not exists(it, k):
                    return
                hp, pt, n = hpar(k), k % PT, tile_of(k) + 1
                if part == 0:
                    pe.wait_ge(pt_hi_ready[pt], transposed(it, k))
                    pe.wait_ge(pt_lo_ready[pt], transposed(it, k))
                    if k % QT == 0:
                        pe.wait_ge(piece_hi_done, pieces(it, k - QT, NP - 1))
                        pe.wait_ge(piece_lo_done, pieces(it, k - QT, NP - 1))
                    if exists(it, k - 1):
                        pe.wait_ge(z_hi_ready, tiles(it, k - 1))
                        pe.wait_ge(z_lo_ready, tiles(it, k - 1))
                for b in (range(0, n // 2), range(n // 2, n))[part]:
                    mm(z_ps[:, 0:P], v_hi[:, hp, b, :], pt_hi[:, pt, b, :], start=(b == 0), stop=False)
                    mm(z_ps[:, 0:P], v_hi[:, hp, b, :], pt_lo[:, pt, b, :], start=False, stop=False)
                    last = mm(z_ps[:, 0:P], v_lo[:, hp, b, :], pt_hi[:, pt, b, :], start=False, stop=(b == n - 1))
                if part == 1:
                    last.then_inc(pv_done, 1)

            def turn_rows(i):
                pe.wait_ge(xn_ready, QT + i + 1)
                if i >= FFN_IN_SLOTS + 2:
                    pe.wait_ge(x2t_ready, i - 1)
                for kd in range(KD):
                    last = nc.tensor.transpose(ffn_banks(i)[0][:, kd * P:(kd + 1) * P],
                                               xn2[:, ORDER[i], kd * P:(kd + 1) * P], ident32[:, :])
                last.then_inc(x2_full, 1)

            def ffn_product(i):
                pe.wait_ge(x2t_ready, i + 1)
                if i >= FFN_IN_SLOTS + 2:
                    pe.wait_ge(res_ready, i - 1)
                for kd in range(KD):
                    last = mm(ffn_banks(i)[1], x2t[:, i % 2, kd, :], f_sum[:, kd, :], start=(kd == 0), stop=(kd == KD - 1))
                last.then_inc(ffn_full, 1)

            def ffn_step(i):
                if i == 0:
                    pe.wait_ge(f_sum_step, R - 1)
                else:
                    ffn_product(i - 1)
                turn_rows(i)

            def scores(it, k):
                if exists(it, k):
                    t, hp = tile_of(k), hpar(k)
                    if k % QT == 0:
                        pe.wait_ge(piece_hi_done, pieces(it, k - QT, KQ_PIECES - 1))
                        pe.wait_ge(piece_lo_done, pieces(it, k - QT, KQ_PIECES - 1))
                    waited = k - QT
                    nb = -(-(t + 1) // TPC)
                    b0 = S_BASE[k % QT]
                    cols = (t + 1) * P
                    tq = slice(t * P, (t + 1) * P)
                    for b in range(nb):
                        f = s_free_after(k, b0 + b)
                        if f > waited and exists(it, f):
                            pe.wait_ge(exp_done, tiles(it, f))
                            waited = f
                        w = min(BANK, cols - b * BANK)
                        ks = slice(b * BANK, b * BANK + w)
                        mm(s_ps[:, b0 + b, 0:w], q_hi[:, hp, tq], k_hi[:, hp, ks], start=True, stop=False)
                        mm(s_ps[:, b0 + b, 0:w], q_hi[:, hp, tq], k_lo[:, hp, ks], start=False, stop=False)
                        last = mm(s_ps[:, b0 + b, 0:w], q_lo[:, hp, tq], k_hi[:, hp, ks], start=False, stop=(b < nb - 1))
                        if b == 1 and nb > 2:
                            last.then_inc(scores_half, 1)
                    w = cols - (nb - 1) * BANK
                    mm(s_ps[:, b0 + nb - 1, w - P:w], ident_b[:, :], mask_b[:, :],
                       start=False, stop=True).then_inc(scores_done, 1)

            def output(it, k):
                ko = k - LAG_OUT
                if exists(it, ko):
                    pe.wait_ge(z_hi_ready, tiles(it, ko))
                    pe.wait_ge(z_lo_ready, tiles(it, ko))
                    if exists(it, ko - 1):
                        pe.wait_ge(acc_added, tiles(it, ko - 1))
                    zp, hp = par(ko), hpar(ko)
                    mm(o_ps[:, 0:D], z_hi[:, zp, :], wo_hi[:, hp, :], start=True, stop=False)
                    mm(o_ps[:, 0:D], z_hi[:, zp, :], wo_lo[:, hp, :], start=False, stop=False)
                    mm(o_ps[:, 0:D], z_lo[:, zp, :], wo_hi[:, hp, :], start=False, stop=True).then_inc(out_full, 1)

            def next_piece(it, k):
                j = piece_of(it, k)
                if j is not None:
                    pe.wait_ge(piece_hi_done, pieces_before(it, k))
                    pe.wait_ge(piece_lo_done, pieces_before(it, k))
                    if j == 0:
                        pe.wait_ge(amax_ready, it * 2 + (k // QT + 2))
                    piece(j)

            def slot(it, k):
                scores(it, k)
                if is_slot(it, k, 0):
                    head0_values()
                next_piece(it, k)
                values(it, k - LAG_PV, 0)
                output(it, k)
                values(it, k - LAG_PV, 1)
                if ffn_step_of(it, k) is not None:
                    ffn_step(ffn_step_of(it, k))

            run_slots(pe, slot)
            ffn_product(FFN_IN_SLOTS - 1)
            pe.wait_ge(exp_done, PAIRS * SLOTS)
            turn_rows(FFN_IN_SLOTS)
            for i in range(FFN_IN_SLOTS, QT):
                if i + 1 < QT:
                    turn_rows(i + 1)
                ffn_product(i)

        @block.scalar
        def _(act):
            def piece_hi(j, hp, full, m_ps=m_ps):
                act.wait_ge(piece_full, full)
                what, c = PIECES[j]
                if what == "max":
                    nc.scalar.copy(amax_t[:, :], m_ps[:, 0:P]).then_inc(piece_hi_done, 1)
                elif what == "spread":
                    nc.scalar.copy(gmax[:, :], m_ps[:, 0:4]).then_inc(piece_hi_done, 1)
                elif what == "wqk":
                    nc.scalar.mul(w_hi[:, 0, :, :], m_ps[:, 0:D], w_scale[:, 0:1])
                    nc.scalar.mul(w_hi[:, 1, :, :], m_ps[:, D:2 * D], w_scale[:, 1:2]).then_inc(piece_hi_done, 1)
                elif what == "wvo":
                    nc.scalar.mul(w_hi[:, 2, :, :], m_ps[:, 0:D], w_scale[:, 2:3])
                    nc.scalar.mul(wo_hi[:, hp, :], m_ps[:, D:2 * D], w_scale[:, 3:4]).then_inc(piece_hi_done, 1)
                else:
                    if what == "v":
                        dst = v_hi[:, hp, c * TPC:(c + 1) * TPC, :]
                    else:
                        dst = (k_hi if what == "k" else q_hi)[:, hp, c * BANK:(c + 1) * BANK]
                    nc.scalar.mul(dst, m_ps[:, :], QKV_DOWN).then_inc(piece_hi_done, 1)

            def xt_hi_part(c):
                for kd in range(KD):
                    act.wait_ge(xt_full, KD * c + kd + 1)
                    nc.scalar.copy(xt_hi[:, kd, c * BANK:(c + 1) * BANK], x_ps[kd][:, :]).then_inc(xt_hi_done, 1)

            def sqrt_var(call, a, b):
                act.wait_ge(var_ready, call + 1)
                nc.scalar.activation(std[:, a:b], var_eps[:, a:b], ACT.Sqrt).then_inc(std_ready, 1)

            def first_std(c):
                sqrt_var(c, c * TPC, (c + 1) * TPC)

            def head0_hi(j):
                piece_hi(j, 0, j + 1, head0_bank(j))

            first_std(0)
            head0_hi(0)
            head0_hi(1)
            first_std(1)
            head0_hi(2)
            xt_hi_part(0)
            first_std(2)
            head0_hi(3)
            xt_hi_part(1)
            head0_hi(4)
            head0_hi(5)
            xt_hi_part(2)
            head0_hi(6)
            head0_hi(7)
            first_std(3)
            head0_hi(8)
            xt_hi_part(3)
            head0_hi(9)
            head0_hi(10)
            head0_hi(11)

            def second_std(n):
                sqrt_var(NC + n, n * LN2_PART, (n + 1) * LN2_PART)

            def x2t_copy(i):
                act.wait_ge(x2_full, i + 1)
                if i < FFN_IN_SLOTS:
                    if i > 0:
                        act.wait_ge(res_ready, i)
                else:
                    act.wait_ge(ffn_full, i - 1)
                nc.scalar.copy(x2t[:, i % 2, :, :], ffn_banks(i)[0]).then_inc(x2t_ready, 1)

            def hi_part(it, k):
                if exists(it, k):
                    w, pp = (tile_of(k) + 1) * P, par(k)
                    act.wait_ge(exp_done, tiles(it, k))
                    if exists(it, k - 2):
                        act.wait_ge(pt_hi_ready[(k - 2) % PT], transposed(it, k - 2))
                    nc.scalar.copy(p_hi[:, pp, 0:w], prob[:, pp, 0:w]).then_inc(p_hi_ready, 1)

            def exponentials(it, k):
                if exists(it, k):
                    w = (tile_of(k) + 1) * P
                    b0, pp = S_BASE[k % QT], par(k)
                    act.wait_ge(bias_ready, tiles(it, k))
                    if exists(it, k - 2):
                        act.wait_ge(p_lo_ready, tiles(it, k - 2))
                    nc.scalar.activation(prob[:, pp, 0:w], s_ps[:, :, :].rearrange("p b n -> p (b n)")[:, b0 * BANK:b0 * BANK + w],
                                         ACT.Exp, bias=exp_bias[:, pp:pp + 1], scale=c_score[:, hpar(k):hpar(k) + 1],
                                         accum_out=row_sum[:, pp:pp + 1]).then_inc(exp_done, 1)

            def next_piece(it, k):
                j = piece_of(it, k)
                if j is not None:
                    piece_hi(j, 1 - hpar(k), pieces(it, k, j))

            def slot(it, k):
                if is_slot(it, k, 0):
                    exponentials(it, k)
                    hi_part(it, k)
                    for j in range(KQ_PIECES, NP):
                        head0_hi(j)
                    next_piece(it, k)
                else:
                    next_piece(it, k)
                    if not is_slot(it, k, LAG_HI):
                        hi_part(it, k - LAG_HI)
                    exponentials(it, k)
                i = ln2_position(it, k)
                if i is not None and i % LN2_PART == 0:
                    second_std(i // LN2_PART)
                    nc.scalar.activation(exp_warm[:, :], ones32[:, 0:1], ACT.Exp)
                if ffn_step_of(it, k) is not None:
                    x2t_copy(ffn_step_of(it, k))

            run_slots(act, slot)
            second_std(QT // LN2_PART - 1)
            for i in range(FFN_IN_SLOTS, QT):
                x2t_copy(i)

        @block.vector
        def _(dve):
            v = nc.vector

            def row_stats(i, t, before):
                v.bn_stats(stats[:, i, :], acc[:, t, :]).then_inc(stats_done, 1)
                dve.wait_ge(stats_done, before + 1)
                v.bn_aggr(mean_var[:, i, :], stats[:, i, :]).then_inc(aggr_done, 1)

            def row_variances(a, b, columns):
                dve.wait_ge(aggr_done, columns)
                v.tensor_scalar(var_eps[:, a:b], mean_var[:, a:b, 1], LN_EPS, None, ALU.add).then_inc(var_ready, 1)

            def first_rstd(call, a, b):
                dve.wait_ge(std_ready, call + 1)
                v.reciprocal(rstd0[:, a:b], std[:, a:b]).then_inc(rstd0_ready, 1)

            def head_amax(count):
                dve.wait_ge(w_loaded, count * 64)
                v.tensor_reduce(amax[:, 0:4], w_raw[:, :, :], AX.X, ALU.max,
                                apply_absolute_value=True).then_inc(amax_ready, 1)

            def head_scales(count, hp):
                n = count * 3 - 3
                v.tensor_scalar(gclamp[:, :], gmax[:, :], 1e-30, None, ALU.max).then_inc(scale_step, 1)
                dve.wait_ge(scale_step, n + 1)
                v.tensor_scalar(pow2[:, :].bitcast(U32), gclamp[:, :].bitcast(U32), EXPONENT_BITS, None,
                                ALU.bitwise_and).then_inc(scale_step, 1)
                dve.wait_ge(scale_step, n + 2)
                v.tensor_scalar(w_inv[:, :], pow2[:, :], 1.0 / W_TOP, None, ALU.mult).then_inc(scale_step, 1)
                dve.wait_ge(scale_step, n + 3)
                v.scalar_tensor_tensor(c_score[:, hp:hp + 1], w_inv[:, 0:1],
                                       float(Dh) ** -0.5 / (X_SCALE * QKV_DOWN) ** 2, w_inv[:, 1:2],
                                       ALU.mult, ALU.mult)
                v.scalar_tensor_tensor(c_out[:, hp:hp + 1], w_inv[:, 2:3], 1.0 / (X_SCALE * QKV_DOWN), w_inv[:, 3:4],
                                       ALU.mult, ALU.mult)
                v.reciprocal(w_scale[:, :], w_inv[:, :]).then_inc(piece_lo_done, 1)

            def piece_lo(j, hp, done, count, m_ps=m_ps):
                dve.wait_ge(piece_hi_done, done)
                what, c = PIECES[j]
                if what == "max":
                    v.tensor_reduce(top[:, :], amax_t[:, :], AX.X, ALU.max).then_inc(top_ready, 1)
                    dve.wait_ge(top_ready, count)
                    v.tensor_scalar(top_diag[:, :], ident32[:, 0:4], top[:, 0:1], None, ALU.mult).then_inc(piece_lo_done, 1)
                    return
                if what == "spread":
                    head_scales(count, hp)
                    return
                if what in ("wqk", "wvo"):
                    for m in range(2):
                        i = 2 * (what == "wvo") + m
                        hi, lo = (wo_hi[:, hp, :], wo_lo[:, hp, :]) if i == 3 else (
                            w_hi[:, i, :, :].rearrange("p k h -> p (k h)"), w_lo[:, i, :, :].rearrange("p k h -> p (k h)"))
                        last = v.scalar_tensor_tensor(lo, m_ps[:, m * D:(m + 1) * D], w_scale[:, i:i + 1], hi,
                                                      ALU.mult, ALU.subtract)
                else:
                    if what == "v":
                        hi, lo = (a[:, hp, c * TPC:(c + 1) * TPC, :].rearrange("p t h -> p (t h)") for a in (v_hi, v_lo))
                    else:
                        hi, lo = (a[:, hp, c * BANK:(c + 1) * BANK] for a in ((k_hi, k_lo) if what == "k" else (q_hi, q_lo)))
                    last = v.scalar_tensor_tensor(lo, m_ps[:, :], QKV_DOWN, hi, ALU.mult, ALU.subtract)
                last.then_inc(piece_lo_done, 1)

            def xt_lo_part(c):
                for kd in range(KD):
                    dve.wait_ge(xt_hi_done, KD * c + kd + 1)
                    v.tensor_tensor(xt_lo[:, kd, c * BANK:(c + 1) * BANK], x_ps[kd][:, :],
                                    xt_hi[:, kd, c * BANK:(c + 1) * BANK], ALU.subtract).then_inc(xt_lo_done, 1)

            def tile_stats(t):
                if t % TPC == 0:
                    dve.wait_ge(x_loaded[t // TPC], 16)
                row_stats(t, t, t)

            def chunk_variances(c):
                row_variances(c * TPC, (c + 1) * TPC, (c + 1) * TPC)

            def chunk_rstd(c):
                first_rstd(c, c * TPC, (c + 1) * TPC)

            def normalise_chunk(c):
                dve.wait_ge(newton_step, 4 * (c + 1))
                for t in range(c * TPC, (c + 1) * TPC):
                    normalise(v, xn, t, t)

            def head0_lo(j):
                piece_lo(j, 0, j + 1, 1, head0_bank(j))

            dve.wait_ge(consts_ready, CONSTS)
            tile_stats(0)
            tile_stats(1)
            tile_stats(2)
            tile_stats(3)
            chunk_variances(0)
            chunk_rstd(0)
            head_amax(1)
            tile_stats(4)
            tile_stats(5)
            head0_lo(0)
            tile_stats(6)
            tile_stats(7)
            chunk_variances(1)
            head0_lo(1)
            normalise_chunk(0)
            chunk_rstd(1)
            tile_stats(8)
            tile_stats(9)
            head0_lo(2)
            normalise_chunk(1)
            xt_lo_part(0)
            tile_stats(10)
            tile_stats(11)
            chunk_variances(2)
            head0_lo(3)
            xt_lo_part(1)
            chunk_rstd(2)
            normalise_chunk(2)
            head0_lo(4)
            head0_lo(5)
            tile_stats(12)
            tile_stats(13)
            tile_stats(14)
            tile_stats(15)
            chunk_variances(3)
            xt_lo_part(2)
            chunk_rstd(3)
            normalise_chunk(3)
            head0_lo(6)
            head0_lo(7)
            head0_lo(8)
            xt_lo_part(3)
            head0_lo(9)
            head0_lo(10)
            head0_lo(11)

            def max_steps(it, k, step):
                return it * (SLOTS + 2 * SPLIT_HEAD) + (k + 1 + (halves(0, k) if step == 2 or tile_of(k) < 2 * TPC else halves(0, k) - 1))

            def second_factors(n):
                a, b = n * LN2_PART, (n + 1) * LN2_PART
                row_variances(a, b, QT + b)
                first_rstd(NC + n, a, b)
                newton(v, dve, NC + n, a, b, 1.0)
                dve.wait_ge(newton_step, 4 * (NC + n + 1))
                if n == 0:
                    dve.wait_ge(f_sum_step, R - 1)

            def result(i):
                dve.wait_ge(ffn_full, i + 1)
                if i + 1 < FFN_IN_SLOTS:
                    dve.wait_ge(x2_full, i + 2)
                dve.wait_ge(resid_ready, i + 1)
                v.scalar_tensor_tensor(res[:, ORDER[i], :], ffn_banks(i)[1], float(R) ** -0.5,
                                       acc[:, ORDER[i], :], ALU.mult, ALU.add).then_inc(res_ready, 1)

            def row_max(it, k):
                if exists(it, k):
                    w, pp, b0 = (tile_of(k) + 1) * P, par(k), S_BASE[k % QT]
                    s_flat = s_ps[:, :, :].rearrange("p b n -> p (b n)")[:, b0 * BANK:b0 * BANK + w]
                    split = 2 * BANK if w > 2 * BANK else 0
                    if split:
                        dve.wait_ge(scores_half, halves(it, k))
                        v.tensor_reduce(neg_max_half[:, pp:pp + 1], s_flat[:, 0:split], AX.X, ALU.max, negate=True)
                    dve.wait_ge(scores_done, tiles(it, k))
                    v.tensor_reduce(neg_max[:, pp:pp + 1], s_flat[:, split:w], AX.X, ALU.max, negate=True).then_inc(max_done, 1)
                    dve.wait_ge(max_done, max_steps(it, k, 1))
                    if split:
                        v.tensor_tensor(neg_max[:, pp:pp + 1], neg_max[:, pp:pp + 1], neg_max_half[:, pp:pp + 1],
                                        ALU.min).then_inc(max_done, 1)
                        dve.wait_ge(max_done, max_steps(it, k, 2))
                    v.tensor_scalar(exp_bias[:, pp:pp + 1], neg_max[:, pp:pp + 1], c_score[:, hpar(k):hpar(k) + 1],
                                    float(np.log(P_SCALE)), ALU.mult, ALU.add).then_inc(bias_ready, 1)

            def accumulate(it, k):
                ko = k - LAG_OUT
                if exists(it, ko):
                    dve.wait_ge(out_full, tiles(it, ko))
                    dve.wait_ge(out_scale_ready, tiles(it, ko))
                    t = tile_of(ko)
                    v.scalar_tensor_tensor(acc[:, t, :], o_ps[:, 0:D], out_scale[:, ko % 8:ko % 8 + 1], acc[:, t, :],
                                           ALU.mult, ALU.add).then_inc(acc_added, 1)
                    if isinstance(it, int) and it * SLOTS + ko >= (H - 1) * QT:
                        dve.wait_ge(acc_added, tiles(it, ko))
                        row_stats(ko % QT, t, QT + ko % QT)

            def z_parts(it, k):
                kh, kv = k - LAG_HI, k - LAG_PV
                if exists(it, kv):
                    zp, down = par(kv), z_down(tile_of(kv))
                    dve.wait_ge(pv_done, tiles(it, kv))
                    v.tensor_scalar(z_hi[:, zp, :], z_ps[:, 0:P], down, None, ALU.mult).then_inc(z_hi_ready, 1)
                if exists(it, kh):
                    dve.wait_ge(exp_done, tiles(it, kh))
                    v.reciprocal(row_rec[:, par(kh):par(kh) + 1], row_sum[:, par(kh):par(kh) + 1]).then_inc(rec_done, 1)
                if exists(it, kv):
                    dve.wait_ge(z_hi_ready, tiles(it, kv))
                    v.scalar_tensor_tensor(z_lo[:, zp, :], z_ps[:, 0:P], down, z_hi[:, zp, :],
                                           ALU.mult, ALU.subtract).then_inc(z_lo_ready, 1)

            def normaliser(it, k):
                kh = k - LAG_HI
                if exists(it, kh):
                    dve.wait_ge(rec_done, tiles(it, kh))
                    v.scalar_tensor_tensor(out_scale[:, kh % 8:kh % 8 + 1], row_rec[:, par(kh):par(kh) + 1],
                                           1.0 / z_down(tile_of(kh)), c_out[:, hpar(kh):hpar(kh) + 1],
                                           ALU.mult, ALU.mult).then_inc(out_scale_ready, 1)

            def next_piece(it, k):
                j = piece_of(it, k)
                if j is not None:
                    piece_lo(j, 1 - hpar(k), pieces(it, k, j), it * 2 + (k // QT + 2))
                if k % QT == QT - 2 and exists(it, k) and not (isinstance(it, int) and 2 * it + k // QT + 2 >= H):
                    head_amax(it * 2 + (k // QT + 3))

            def slot(it, k):
                row_max(it, k)
                if is_slot(it, k, 0):
                    for j in range(KQ_PIECES, NP):
                        head0_lo(j)
                    head_amax(2)
                next_piece(it, k)
                accumulate(it, k)
                z_parts(it, k)
                normaliser(it, k)
                if ffn_step_of(it, k) not in (None, 0):
                    result(ffn_step_of(it, k) - 1)
                i = ln2_position(it, k)
                if i is not None:
                    if i % LN2_PART == 0:
                        second_factors(i // LN2_PART)
                    normalise(v, xn2, i, ORDER[i])

            run_slots(dve, slot)

            second_factors(QT // LN2_PART - 1)
            for i in range(QT - LN2_PART, QT):
                normalise(v, xn2, i, ORDER[i])
            for i in range(FFN_IN_SLOTS, QT + 1):
                result(i - 1)


_INS = ["L0_attn_x", "L0_attn_W_K", "L0_attn_W_Q", "L0_attn_W_V", "L0_attn_W_O", "L0_ffn_factors", "L0_ffn_bias"]


def kernel(**inputs):
    from concourse.bacc import Bacc
    from concourse.bass_utils import run_bass_kernel_spmd

    nc = Bacc("TRN2", target_bir_lowering=False, num_devices=1)
    arrays, args = {}, []
    for name in _INS:
        a = np.ascontiguousarray(inputs[name])
        arrays[f"in_{name}"] = a
        args.append(nc.dram_tensor(f"in_{name}", a.shape, mybir.dt.from_np(a.dtype), kind="ExternalInput").ap())
    out = nc.dram_tensor("out_x", inputs["L0_attn_x"].shape, F32, kind="ExternalOutput").ap()
    preln_attention_ffn(nc, *args, out)
    r = run_bass_kernel_spmd(nc, [arrays], core_ids=[0])
    return r.results[0]["out_x"]
```
